# Optimizing a Trainium2 kernel written in Bass

```python
import numpy as np
import jax
import jax.numpy as jnp

def _softmax(x, axis=-1):
    return jax.nn.softmax(x, axis=axis)

def _gelu(x):
    return jax.nn.gelu(x, approximate=True)

def _silu(x):
    return jax.nn.silu(x)

def _sigmoid(x):
    return jax.nn.sigmoid(x)

def _layernorm(x, axis=-1, eps=1e-05):
    m = jnp.mean(x, axis=axis, keepdims=True)
    v = jnp.var(x, axis=axis, keepdims=True)
    return (x - m) / jnp.sqrt(v + eps)

def _scatter_add(tgt, idx, src, axis=0):
    return tgt.at[idx].add(src)

def _segment_sum(src, seg, n):
    return jax.ops.segment_sum(src, seg, n)
kernel_name = 'mk_hybrid_d1_jaxref_r8_c72d1b'

def setup_inputs(seed: int=0):
    np.random.seed(seed)
    _w = jnp.asarray

    def _L0_attn_a_setup():
        import jax, jax.numpy as jnp
        import numpy as np
        B_SZ, SEQ, D_MODEL = (2, 64, 128)
        EXPAND, HEAD_DIM = (2, 64)
        D_INNER = EXPAND * D_MODEL
        N_HEADS = D_INNER // HEAD_DIM
        D_STATE = 64
        EPS = 1e-06
        PROJ_DIM = 2 * D_INNER + 2 * N_HEADS * D_STATE + N_HEADS

        def _rope(x, theta):
            x0, x1 = (x[..., 0::2], x[..., 1::2])
            c, s = (jnp.cos(theta), jnp.sin(theta))
            y = jnp.stack([x0 * c - x1 * s, x0 * s + x1 * c], axis=-1)
            return y.reshape(x.shape)
        key = jax.random.key(seed)
        k = jax.random.split(key, 5)
        return {'hidden': jax.random.normal(k[0], (B_SZ, SEQ, D_MODEL), jnp.float32), 'W_in': 0.02 * jax.random.normal(k[1], (D_MODEL, PROJ_DIM), jnp.float32), 'dt_bias': 0.5 * jax.random.normal(k[2], (N_HEADS,), jnp.float32), 'A_log': 0.5 * jax.random.normal(k[3], (N_HEADS,), jnp.float32), 'norm_weight': jnp.ones((D_INNER,), jnp.float32), 'W_out': 0.02 * jax.random.normal(k[4], (D_INNER, D_MODEL), jnp.float32)}
    _L0_attn_a_in = _L0_attn_a_setup()

    def _L0_attn_b_setup():
        import jax, jax.numpy as jnp
        import numpy as np
        from jax import lax
        D_MODEL = 128
        EXPAND = 2
        D_INNER = EXPAND * D_MODEL
        D_STATE = 16
        D_CONV = 4
        DT_RANK = D_MODEL // 16
        B_SZ = 4
        SEQ = 256

        def _mamba_fwd(x, W_in, conv_w, conv_b, W_x, W_dt, b_dt, A_log, D, W_out):
            B, L, _ = x.shape
            xz = jnp.einsum('bld,ed->ble', x, W_in)
            u, z = jnp.split(xz, 2, axis=-1)
            u_nc = u.transpose(0, 2, 1)
            u_c = lax.conv_general_dilated(u_nc, conv_w[:, None, :], window_strides=(1,), padding=[(D_CONV - 1, 0)], feature_group_count=D_INNER, dimension_numbers=('NCH', 'OIH', 'NCH'))
            u_c = (u_c + conv_b[None, :, None]).transpose(0, 2, 1)
            u_c = jax.nn.silu(u_c)
            x_dbl = jnp.einsum('bld,ed->ble', u_c, W_x)
            dt_r, Bm, Cm = jnp.split(x_dbl, [DT_RANK, DT_RANK + D_STATE], axis=-1)
            dt = jax.nn.softplus(jnp.einsum('blr,dr->bld', dt_r, W_dt) + b_dt)
            A = -jnp.exp(A_log)

            def step(h, inp):
                dt_t, u_t, B_t, C_t = inp
                dA = jnp.exp(dt_t[..., None] * A)
                h = dA * h + (dt_t * u_t)[..., None] * B_t[:, None, :]
                y_t = jnp.einsum('bds,bs->bd', h, C_t)
                return (h, y_t)
            xs = (dt.transpose(1, 0, 2), u_c.transpose(1, 0, 2), Bm.transpose(1, 0, 2), Cm.transpose(1, 0, 2))
            h0 = jnp.zeros((B, D_INNER, D_STATE), dtype=x.dtype)
            _, ys = lax.scan(step, h0, xs)
            y = ys.transpose(1, 0, 2)
            y = y + u_c * D
            y = y * jax.nn.silu(z)
            out = jnp.einsum('bld,ed->ble', y, W_out)
            return out

        def _reference_tuple_inner(x, W_in, conv_w, conv_b, W_x, W_dt, b_dt, A_log, D, W_out):
            out = _mamba_fwd(x, W_in, conv_w, conv_b, W_x, W_dt, b_dt, A_log, D, W_out)
            return (out, None)
        key = jax.random.key(seed)
        ks = jax.random.split(key, 10)
        s = lambda k, shape, scale: jax.random.normal(k, shape, dtype=jnp.float32) * scale
        inp = {'x': s(ks[0], (B_SZ, SEQ, D_MODEL), 1.0), 'W_in': s(ks[1], (2 * D_INNER, D_MODEL), D_MODEL ** (-0.5)), 'conv_w': s(ks[2], (D_INNER, D_CONV), D_CONV ** (-0.5)), 'conv_b': s(ks[3], (D_INNER,), 0.02), 'W_x': s(ks[4], (DT_RANK + 2 * D_STATE, D_INNER), D_INNER ** (-0.5)), 'W_dt': s(ks[5], (D_INNER, DT_RANK), DT_RANK ** (-0.5)), 'b_dt': s(ks[6], (D_INNER,), 0.5), 'A_log': jnp.log(jnp.broadcast_to(jnp.arange(1, D_STATE + 1, dtype=jnp.float32), (D_INNER, D_STATE))), 'D': jnp.ones((D_INNER,), dtype=jnp.float32), 'W_out': s(ks[7], (D_MODEL, D_INNER), D_INNER ** (-0.5))}
        return inp
    _L0_attn_b_in = _L0_attn_b_setup()

    def _L0_ffn_setup():
        import jax, jax.numpy as jnp
        import numpy as np
        B, S, H = (2, 256, 128)
        N, F, SF, K = (16, 128, 512, 1)
        key = jax.random.key(seed)
        ks = jax.random.split(key, 7)
        std = 0.02
        return {'hidden_states': jax.random.normal(ks[0], (B, S, H), dtype=jnp.float32), 'router_w': jax.random.normal(ks[1], (N, H), dtype=jnp.float32) * std, 'gate_up_proj': jax.random.normal(ks[2], (N, H, 2 * F), dtype=jnp.float32) * std, 'down_proj': jax.random.normal(ks[3], (N, F, H), dtype=jnp.float32) * std, 'shared_gate_w': jax.random.normal(ks[4], (SF, H), dtype=jnp.float32) * std, 'shared_up_w': jax.random.normal(ks[5], (SF, H), dtype=jnp.float32) * std, 'shared_down_w': jax.random.normal(ks[6], (H, SF), dtype=jnp.float32) * std}
    _L0_ffn_in = _L0_ffn_setup()
    _d = {'L0_attn_a_hidden': _L0_attn_a_in['hidden'], 'L0_attn_a_W_in': _L0_attn_a_in['W_in'], 'L0_attn_a_dt_bias': _L0_attn_a_in['dt_bias'], 'L0_attn_a_A_log': _L0_attn_a_in['A_log'], 'L0_attn_a_norm_weight': _L0_attn_a_in['norm_weight'], 'L0_attn_a_W_out': _L0_attn_a_in['W_out'], 'L0_attn_b_W_in': _L0_attn_b_in['W_in'], 'L0_attn_b_conv_w': _L0_attn_b_in['conv_w'], 'L0_attn_b_conv_b': _L0_attn_b_in['conv_b'], 'L0_attn_b_W_x': _L0_attn_b_in['W_x'], 'L0_attn_b_W_dt': _L0_attn_b_in['W_dt'], 'L0_attn_b_b_dt': _L0_attn_b_in['b_dt'], 'L0_attn_b_A_log': _L0_attn_b_in['A_log'], 'L0_attn_b_D': _L0_attn_b_in['D'], 'L0_attn_b_W_out': _L0_attn_b_in['W_out'], 'L0_ffn_router_w': _L0_ffn_in['router_w'], 'L0_ffn_gate_up_proj': _L0_ffn_in['gate_up_proj'], 'L0_ffn_down_proj': _L0_ffn_in['down_proj'], 'L0_ffn_shared_gate_w': _L0_ffn_in['shared_gate_w'], 'L0_ffn_shared_up_w': _L0_ffn_in['shared_up_w'], 'L0_ffn_shared_down_w': _L0_ffn_in['shared_down_w']}
    _x0 = _d['L0_attn_a_hidden']
    _d['L0_attn_a_hidden'] = jax.random.normal(jax.random.fold_in(jax.random.key(seed), 1), (8, 256, 128), dtype=_x0.dtype)
    del _x0
    return _d

def reference(L0_attn_a_hidden, L0_attn_a_W_in, L0_attn_a_dt_bias, L0_attn_a_A_log, L0_attn_a_norm_weight, L0_attn_a_W_out, L0_attn_b_W_in, L0_attn_b_conv_w, L0_attn_b_conv_b, L0_attn_b_W_x, L0_attn_b_W_dt, L0_attn_b_b_dt, L0_attn_b_A_log, L0_attn_b_D, L0_attn_b_W_out, L0_ffn_router_w, L0_ffn_gate_up_proj, L0_ffn_down_proj, L0_ffn_shared_gate_w, L0_ffn_shared_up_w, L0_ffn_shared_down_w):

    def _L0_attn_a_ref(hidden, W_in, dt_bias, A_log, norm_weight, W_out):
        import jax, jax.numpy as jnp
        import numpy as np
        B_SZ, SEQ, D_MODEL = (2, 64, 128)
        EXPAND, HEAD_DIM = (2, 64)
        D_INNER = EXPAND * D_MODEL
        N_HEADS = D_INNER // HEAD_DIM
        D_STATE = 64
        EPS = 1e-06
        PROJ_DIM = 2 * D_INNER + 2 * N_HEADS * D_STATE + N_HEADS

        def _rope(x, theta):
            x0, x1 = (x[..., 0::2], x[..., 1::2])
            c, s = (jnp.cos(theta), jnp.sin(theta))
            y = jnp.stack([x0 * c - x1 * s, x0 * s + x1 * c], axis=-1)
            return y.reshape(x.shape)
        b, l, _ = hidden.shape
        proj = hidden @ W_in
        hn = N_HEADS * D_STATE
        z = proj[..., :D_INNER]
        xr = proj[..., D_INNER:2 * D_INNER].reshape(b, l, N_HEADS, HEAD_DIM)
        Bm = proj[..., 2 * D_INNER:2 * D_INNER + hn].reshape(b, l, N_HEADS, D_STATE)
        Cm = proj[..., 2 * D_INNER + hn:2 * D_INNER + 2 * hn].reshape(b, l, N_HEADS, D_STATE)
        dt = jax.nn.softplus(proj[..., -N_HEADS:] + dt_bias)
        A = -jnp.exp(A_log)
        alpha = jnp.exp(dt * A)
        beta = 0.5 * dt * alpha
        gamma = 0.5 * dt
        half = D_STATE // 2
        inv_freq = 1.0 / 10000.0 ** (jnp.arange(half, dtype=jnp.float32) / half)
        theta = jnp.cumsum(dt, axis=1)[..., None] * inv_freq
        Bm = _rope(Bm, theta)
        Cm = _rope(Cm, theta)
        Bp = jnp.pad(Bm[:, :-1], ((0, 0), (1, 0), (0, 0), (0, 0)))
        xp = jnp.pad(xr[:, :-1], ((0, 0), (1, 0), (0, 0), (0, 0)))
        tl = lambda t: jnp.moveaxis(t, 1, 0)
        xs = (tl(xr), tl(Bm), tl(Cm), tl(Bp), tl(xp), tl(alpha), tl(beta), tl(gamma))
        h0 = jnp.zeros((b, N_HEADS, D_STATE, HEAD_DIM), hidden.dtype)

        def step(h, inp):
            x_t, B_t, C_t, Bprev, xprev, a, bt, g = inp
            h = a[..., None, None] * h + bt[..., None, None] * jnp.einsum('bhn,bhp->bhnp', Bprev, xprev) + g[..., None, None] * jnp.einsum('bhn,bhp->bhnp', B_t, x_t)
            y = jnp.einsum('bhn,bhnp->bhp', C_t, h)
            return (h, y)
        _, ys = jax.lax.scan(step, h0, xs)
        y = jnp.moveaxis(ys, 0, 1).reshape(b, l, D_INNER)
        y = y * jax.nn.silu(z)
        rms = jnp.sqrt(jnp.mean(y * y, axis=-1, keepdims=True) + EPS)
        y = y / rms * norm_weight
        return y @ W_out

    def _L0_attn_b_ref(x, W_in, conv_w, conv_b, W_x, W_dt, b_dt, A_log, D, W_out):
        import jax, jax.numpy as jnp
        import numpy as np
        from jax import lax
        D_MODEL = 128
        EXPAND = 2
        D_INNER = EXPAND * D_MODEL
        D_STATE = 16
        D_CONV = 4
        DT_RANK = D_MODEL // 16
        B_SZ = 4
        SEQ = 256

        def _mamba_fwd(x, W_in, conv_w, conv_b, W_x, W_dt, b_dt, A_log, D, W_out):
            B, L, _ = x.shape
            xz = jnp.einsum('bld,ed->ble', x, W_in)
            u, z = jnp.split(xz, 2, axis=-1)
            u_nc = u.transpose(0, 2, 1)
            u_c = lax.conv_general_dilated(u_nc, conv_w[:, None, :], window_strides=(1,), padding=[(D_CONV - 1, 0)], feature_group_count=D_INNER, dimension_numbers=('NCH', 'OIH', 'NCH'))
            u_c = (u_c + conv_b[None, :, None]).transpose(0, 2, 1)
            u_c = jax.nn.silu(u_c)
            x_dbl = jnp.einsum('bld,ed->ble', u_c, W_x)
            dt_r, Bm, Cm = jnp.split(x_dbl, [DT_RANK, DT_RANK + D_STATE], axis=-1)
            dt = jax.nn.softplus(jnp.einsum('blr,dr->bld', dt_r, W_dt) + b_dt)
            A = -jnp.exp(A_log)

            def step(h, inp):
                dt_t, u_t, B_t, C_t = inp
                dA = jnp.exp(dt_t[..., None] * A)
                h = dA * h + (dt_t * u_t)[..., None] * B_t[:, None, :]
                y_t = jnp.einsum('bds,bs->bd', h, C_t)
                return (h, y_t)
            xs = (dt.transpose(1, 0, 2), u_c.transpose(1, 0, 2), Bm.transpose(1, 0, 2), Cm.transpose(1, 0, 2))
            h0 = jnp.zeros((B, D_INNER, D_STATE), dtype=x.dtype)
            _, ys = lax.scan(step, h0, xs)
            y = ys.transpose(1, 0, 2)
            y = y + u_c * D
            y = y * jax.nn.silu(z)
            out = jnp.einsum('bld,ed->ble', y, W_out)
            return out

        def _reference_tuple_inner(x, W_in, conv_w, conv_b, W_x, W_dt, b_dt, A_log, D, W_out):
            out = _mamba_fwd(x, W_in, conv_w, conv_b, W_x, W_dt, b_dt, A_log, D, W_out)
            return (out, None)
        return _reference_tuple_inner(x, W_in, conv_w, conv_b, W_x, W_dt, b_dt, A_log, D, W_out)[0]

    def _L0_ffn_ref(hidden_states, router_w, gate_up_proj, down_proj, shared_gate_w, shared_up_w, shared_down_w):
        import jax, jax.numpy as jnp
        import numpy as np
        B, S, H = (2, 256, 128)
        N, F, SF, K = (16, 128, 512, 1)
        b, s, h = hidden_states.shape
        hidden = hidden_states.reshape(-1, h)
        t = hidden.shape[0]
        logits = hidden @ router_w.T
        top_vals, top_idx = jax.lax.top_k(logits, K)
        scores = jnp.full_like(logits, -jnp.inf)
        scores = scores.at[jnp.arange(t)[:, None], top_idx].set(top_vals)
        scores = jax.nn.sigmoid(scores.astype(jnp.float32)).astype(hidden.dtype)
        routed_in = hidden[None, :, :] * scores.T[:, :, None]
        gate_up = jnp.einsum('nth,nhf->ntf', routed_in, gate_up_proj)
        gate, up = jnp.split(gate_up, 2, axis=-1)
        routed_out = jnp.einsum('ntf,nfh->nth', up * jax.nn.silu(gate), down_proj)
        expert_sum = routed_out.sum(axis=0)
        shared = jax.nn.silu(hidden @ shared_gate_w.T) * (hidden @ shared_up_w.T) @ shared_down_w.T
        return (shared + expert_sum).reshape(b, s, h)
    x = L0_attn_a_hidden
    x = x + _L0_attn_a_ref(_layernorm(x, axis=-1), L0_attn_a_W_in, L0_attn_a_dt_bias, L0_attn_a_A_log, L0_attn_a_norm_weight, L0_attn_a_W_out)
    x = x + _L0_ffn_ref(_layernorm(x, axis=-1), L0_ffn_router_w, L0_ffn_gate_up_proj, L0_ffn_down_proj, L0_ffn_shared_gate_w, L0_ffn_shared_up_w, L0_ffn_shared_down_w)
    x = x + _L0_attn_b_ref(_layernorm(x, axis=-1), L0_attn_b_W_in, L0_attn_b_conv_w, L0_attn_b_conv_b, L0_attn_b_W_x, L0_attn_b_W_dt, L0_attn_b_b_dt, L0_attn_b_A_log, L0_attn_b_D, L0_attn_b_W_out)
    x = x + _L0_ffn_ref(_layernorm(x, axis=-1), L0_ffn_router_w, L0_ffn_gate_up_proj, L0_ffn_down_proj, L0_ffn_shared_gate_w, L0_ffn_shared_up_w, L0_ffn_shared_down_w)
    return x

_drawn_inputs = setup_inputs


def setup_inputs(seed=0):
    import zlib

    import numpy as np

    out = dict(_drawn_inputs(seed))
    spreads = {'L0_attn_a_norm_weight': (1.0, 0.2), 'L0_attn_b_D': (1.0, 0.2)}
    factors = {'L0_attn_b_conv_b': 3.298,
     'L0_ffn_router_w': 8.0,
     'L0_ffn_gate_up_proj': 8.0,
     'L0_ffn_down_proj': 8.0,
     'L0_ffn_shared_gate_w': 2.773,
     'L0_ffn_shared_up_w': 2.715,
     'L0_ffn_shared_down_w': 2.683}
    for name, (base, spread) in spreads.items():
        noise = np.random.default_rng([zlib.crc32(name.encode()), seed]).standard_normal(out[name].shape)
        drawn = base * np.exp(spread * noise) if base else spread * noise
        out[name] = jnp.asarray(drawn.astype(out[name].dtype))
    for name, factor in factors.items():
        out[name] = (out[name] * factor).astype(out[name].dtype)
    return out
```

```python
from contextlib import ExitStack

import numpy as np
import concourse.bass as bass
from concourse import mybir

F32, BF16, I32, U16 = mybir.dt.float32, mybir.dt.bfloat16, mybir.dt.int32, mybir.dt.uint16
ALU, ACT, AX = mybir.AluOpType, mybir.ActivationFunctionType, mybir.AxisListType

P = 128
BATCH, SEQ, DM = 8, 256, 128
NBLK = BATCH * SEQ // P
NTOK = BATCH * SEQ
BANK = 512
NGRP = NTOK // BANK
GB = BANK // P
NH, HD, NS = 4, 64, 64
HALF = NS // 2
NPAIR = NH * HD // P
NE, EF, SF = 16, 128, 512
NSC = SF // P
NSLOT = NBLK + NE - 1
DI, DS, DC, DR = 256, 16, 4, 8
NCH = DI // P
PADT = SEQ + DC - 1
HTOK = NTOK // 2
ROUND = 1.5 * 2.0 ** 23
MASKED = -1e30

_W_EARLY = [("in_a", 1028), ("dt_bias", NH), ("a_log_a", NH), ("ident", P), ("tri", 2 * P), ("shift", P),
            ("shift_in", P), ("inv_freq", HALF), ("norm_w", NPAIR), ("out_a", NPAIR * DM)]
_W_LATE = [("router", NE), ("shared_gate", SF), ("shared_up", SF), ("shared_down", NSC * DM),
           ("gate_up", NE * 2 * EF), ("down", NE * DM), ("rev_expert", NE), ("keep", NE * NBLK), ("slot", NSLOT),
           ("in_b", 2 * DI), ("conv_w", DC * DI), ("conv_b", NCH), ("x_b", NCH * (2 * DS + DR)), ("dt_w", DI),
           ("dt_b", NCH), ("a_log_b", NCH * DS), ("d_b", NCH), ("out_b", NCH * DM)]
_C16 = [("ident16", P), ("tri16", P), ("ones16", P), ("mask16", 3 * P), ("pick_head", NH * P),
        ("pick_row", 2 * DS * P)]


def offsets(table):
    at, found = 0, {}
    for name, width in table:
        found[name] = (at, width)
        at += width
    return found, at


W_AT, W_COLS = offsets(_W_EARLY + _W_LATE)
W_EARLY_COLS = offsets(_W_EARLY)[1]
C_AT, C_COLS = offsets(_C16)


class Engine:

    def __init__(self, engine, semaphore):
        self.engine, self.semaphore, self.count, self.seen = engine, semaphore, 0, {}

    def after(self, *marks):
        for mark in marks:
            if isinstance(mark, list):
                self.after(*mark)
            elif mark is not None and self.seen.get(mark[0].name, 0) < mark[1]:
                self.engine.wait_ge(mark[0], mark[1])
                self.seen[mark[0].name] = mark[1]
        return self.engine

    def did(self, instruction):
        instruction.then_inc(self.semaphore, 1)
        self.count += 1
        return self.last()

    def last(self):
        return (self.semaphore, self.count)


class Transfers:

    def __init__(self, semaphore):
        self.semaphore, self.count = semaphore, 0

    def sent(self, dma):
        dma.then_inc(self.semaphore, 16)
        self.count += 16
        return (self.semaphore, self.count)

    def last(self):
        return (self.semaphore, self.count)


class Ring:

    def __init__(self, banks):
        self.banks, self.freed, self.turn = banks, [None] * len(banks), 0

    def take(self):
        self.turn += 1
        return self.banks[(self.turn - 1) % len(self.banks)], self.freed[(self.turn - 1) % len(self.banks)]

    def release(self, bank, mark):
        self.freed[self.banks.index(bank)] = mark


def build(nc, x_in, w_in, c_in, out):
    with ExitStack() as stack:
        def sb(name, shape, dtype=F32):
            return stack.enter_context(nc.sbuf_tensor(name, shape, dtype))

        def sem(name):
            return stack.enter_context(nc.semaphore(name))

        pe, dve = Engine(nc.tensor, sem("pe_done")), Engine(nc.vector, sem("dve_done"))
        act, pool = Engine(nc.scalar, sem("act_done")), Engine(nc.gpsimd, sem("pool_done"))
        sp = Engine(nc.sync, sem("sp_done"))

        psum = stack.enter_context(nc.psum_tensor("psum", [P, 8, BANK], F32))
        x = sb("x", [P, NBLK, DM])
        xn = sb("xn", [P, NBLK, DM])
        xnt = sb("xnt", [P, BATCH, PADT])
        w = sb("w", [P, W_COLS])
        c16 = sb("c16", [P, C_COLS], BF16)
        stats = sb("stats", [P, NBLK, 6])
        moments = sb("moments", [P, NBLK, 2])
        deviation = sb("deviation", [P, NBLK])
        rstd = sb("rstd", [P, NBLK])
        consts = sb("consts", [P, 4])
        zeros = sb("zeros", [P, DM])
        ARENA = 30000
        arena = sb("arena", [P, ARENA])
        sorted_x = [nc.dram_tensor(f"sorted_x{i}", [NSLOT * P, DM], F32, kind="Internal").ap() for i in range(2)]
        sorted_y = [nc.dram_tensor(f"sorted_y{i}", [NSLOT * P, DM], F32, kind="Internal").ap() for i in range(2)]

        def wt(name, rows=slice(0, P)):
            at, width = W_AT[name]
            return w[rows, at:at + width]

        def ct(name, rows=slice(0, P)):
            at, width = C_AT[name]
            return c16[rows, at:at + width]

        eps_ln, eps_rms, quarter_turn, one = (consts[:, i:i + 1] for i in range(4))
        ident, tri = wt("ident"), wt("tri")
        x_cols = x[:].rearrange("p b c -> p (b c)")
        xnt_tokens = xnt[:, :, DC - 1:PADT]

        def xnt_block(j):
            return xnt[:, j // 2, DC - 1 + P * (j % 2):DC - 1 + P * (j % 2) + P]

        def xnt_group(g):
            return xnt_tokens[:, 2 * g:2 * g + 2, :]

        load_x, load_early, load_late = Transfers(sem("load_x")), Transfers(sem("load_early")), Transfers(sem("load_late"))
        zero_fill = Transfers(sem("zero_fill"))
        load_x.sent(nc.sync.dma_start(x_cols, x_in))
        load_early.sent(nc.scalar.dma_start(w[:, 0:W_EARLY_COLS], w_in[:, 0:W_EARLY_COLS]))
        load_early.sent(nc.scalar.dma_start(c16[:].bitcast(U16), c_in))
        load_late.sent(nc.sync.dma_start(w[:, W_EARLY_COLS:W_COLS], w_in[:, W_EARLY_COLS:W_COLS]))
        zeroed = dve.did(nc.vector.memset(zeros[:], 0.0))
        for buffer in sorted_x:
            zero_fill.sent(sp.after(zeroed).dma_start(buffer.rearrange("(s p) c -> p s c", p=P),
                                        zeros[:].unsqueeze(1).to_broadcast([P, NSLOT, DM])))
        for value, tile in ((1e-5, eps_ln), (1e-6, eps_rms), (float(np.pi / 2), quarter_turn), (1.0, one)):
            consts_set = pool.did(nc.gpsimd.memset(tile, value))
        pads_set = pool.did(nc.gpsimd.memset(xnt[:, :, 0:DC - 1], 0.0))
        for e in (pe, dve, act, pool):
            e.after(load_early.last(), consts_set, pads_set)

        def next_layer(*more):
            marks = [e.last() for e in (pe, dve, act, pool)] + list(more)
            for e in (pe, dve, act, pool):
                e.after(marks)

        def carve():
            taken = [0]

            def piece(columns, rows=slice(0, P)):
                taken[0] += columns
                assert taken[0] <= ARENA, taken
                return arena[rows, taken[0] - columns:taken[0]]
            return piece

        def normalise(ready):
            dve.after(ready)
            for j in range(NBLK):
                stat = dve.did(nc.vector.bn_stats(stats[:, j, :], x[:, j, :]))
            dve.after(stat)
            for j in range(NBLK):
                moment = dve.did(nc.vector.bn_aggr(moments[:, j, :], stats[:, j, :]))
            root = act.did(act.after(moment).activation(deviation[:], moments[:, :, 1], ACT.Sqrt, bias=eps_ln))
            inverse = dve.did(dve.after(root).reciprocal(rstd[:], deviation[:]))
            dve.after(inverse)
            ring = Ring([psum[:, i, :] for i in range(2)])
            marks = []
            for g in range(NGRP):
                for j in range(GB * g, GB * g + GB):
                    scaled = dve.did(nc.vector.tensor_scalar(xn[:, j, :], x[:, j, :], moments[:, j, 0:1], rstd[:, j:j + 1],
                                                             ALU.subtract, ALU.mult))
                bank = psum[:, g % 2, :]
                pe.after(scaled, marks[g - 2] if g >= 2 else None)
                for j in range(GB):
                    turned = pe.did(nc.tensor.transpose(bank[:, P * j:P * j + P], xn[:, GB * g + j, :], ident))
                marks.append(act.did(act.after(turned).activation(
                    xnt_group(g), bank.rearrange("p (s t) -> p s t", s=2), ACT.Copy)))
            return marks

        def state_space():
            piece = carve()
            z_silu = piece(NPAIR * NTOK).rearrange("p (c t) -> p c t", c=NPAIR)
            xw = piece(NBLK * NH * HD).rearrange("p (j h c) -> p j h c", j=NBLK, h=NH)
            rotated = [[piece(NTOK) for _ in range(2)] for _ in range(2)]
            cosine, sine = piece(NTOK), piece(NTOK)
            gated = cosine_and_sine = None
            dt = piece(NBLK * NH)
            small = [piece(NBLK * NH) for _ in range(8)]
            cum = piece(NBLK * NH)
            neg_cum, neg_u = piece(NBLK * NH), piece(NBLK * NH)
            a_row = piece(NH)
            parts = piece(NBLK * 3 * NH // 2).bitcast(BF16).rearrange("p (j q h) -> p j q h", j=NBLK, q=3)
            cum_parts = piece(NTOK // 2, slice(0, 3 * NH)).bitcast(BF16)
            products = [piece(BANK) for _ in range(8)]
            decay = [piece(3 * P) for _ in range(3)]
            mixed = [piece(3 * P) for _ in range(3)]
            out_w = piece(NPAIR * DM)
            freq_dt = xw.rearrange("p j h c -> p (j h c)")[:, 0:NTOK]
            turns = xw.rearrange("p j h c -> p (j h c)")[:, NTOK:2 * NTOK]
            n4 = NBLK * NH

            normed = normalise(load_x.last())
            in_a = wt("in_a")
            z_w, bc_w = in_a[:, 0:2 * P], in_a[:, 2 * P:6 * P]
            xr_w, dt_w = in_a[:, 6 * P:8 * P], in_a[:, 8 * P:8 * P + NH]

            dt_bank, aux_bank = psum[:, 2, 0:n4], psum[:, 3, :]
            pe.after(normed)
            for j in range(NBLK):
                raw_ready = pe.did(nc.tensor.matmul(dt_bank[:, NH * j:NH * j + NH], xnt_block(j), dt_w, start=True, stop=True))
            v, least, e, log1p, shifted, total, inverse, half = small

            def heads(t):
                return t.rearrange("p (j h) -> p j h", h=NH)

            def per_head(row):
                return row.unsqueeze(1).to_broadcast([P, NBLK, NH])

            m = dve.did(dve.after(raw_ready).tensor_tensor(heads(v), heads(dt_bank), per_head(wt("dt_bias")), ALU.add))
            m = dve.did(dve.after(m).scalar_tensor_tensor(least, v, -1.0, v, ALU.mult, ALU.min))
            e_ready = act.did(act.after(m).activation(e, least, ACT.Exp))
            a_exp = act.did(nc.scalar.activation(a_row, wt("a_log_a"), ACT.Exp))
            log_ready = act.did(act.after(e_ready).activation(log1p, e, ACT.Ln, bias=one))
            dt_ready = dve.did(dve.after(log_ready).scalar_tensor_tensor(dt, v, 0.0, log1p, ALU.max, ALU.add))
            neg_dta = half
            m = dve.did(dve.after(a_exp, dt_ready).tensor_tensor(heads(neg_dta), heads(dt), per_head(a_row), ALU.mult))
            pe.after(m)
            nxt, run = aux_bank[:, 0:n4], aux_bank[:, n4:2 * n4]
            odd_dt, even_cols = heads(dt)[:, 1::2, :], heads(nxt)[:, 0::2, :]
            nc.tensor.matmul(nxt, wt("shift"), dt, start=True, stop=True)
            nc.tensor.matmul(even_cols, wt("shift_in"), odd_dt, start=False, stop=True, skip_group_check=True)
            nc.tensor.matmul(run, tri[:, 0:P], neg_dta, start=False, stop=True, skip_group_check=True)
            sums = pe.did(nc.tensor.matmul(heads(run)[:, 1::2, :], tri[:, P:2 * P], heads(neg_dta)[:, 0::2, :],
                                           start=False, stop=True, skip_group_check=True))
            dve.after(sums)
            m_shift = dve.did(nc.vector.tensor_copy(shifted, nxt))
            m_neg = dve.did(nc.vector.tensor_copy(neg_cum, run))
            m_cum = dve.did(nc.vector.tensor_scalar(cum, run, -1.0, None, ALU.mult))
            m_tot = dve.did(dve.after(m_shift).tensor_tensor(total, dt, shifted, ALU.add))
            m = dve.did(dve.after(m_tot).tensor_scalar(e, total, 1e-30, None, ALU.max))
            m = dve.did(dve.after(m).reciprocal(inverse, e))
            m_u = dve.did(dve.after(m).scalar_tensor_tensor(neg_u, shifted, -1.0, inverse, ALU.mult, ALU.mult))
            weight_ready = dve.did(nc.vector.tensor_scalar(v, total, 0.5, None, ALU.mult))
            parts_of = parts
            m1 = dve.did(dve.after(m_cum).tensor_copy(parts_of[:, :, 0, :], heads(cum)))
            m2 = dve.did(dve.after(m1).tensor_tensor(heads(log1p), heads(cum), parts_of[:, :, 0, :], ALU.subtract))
            m3 = dve.did(dve.after(m2).tensor_copy(parts_of[:, :, 1, :], heads(log1p)))
            m4 = dve.did(dve.after(m3).tensor_tensor(parts_of[:, :, 2, :], heads(log1p), parts_of[:, :, 1, :], ALU.subtract))
            pe.after(m4)
            for k in range(2):
                for j in range(8):
                    t = psum[:, 4 + k, :].bitcast(BF16)[0:3 * NH, P * j:P * j + P]
                    turned = pe.did(nc.tensor.transpose(t, parts_of[:, 8 * k + j, :, :].rearrange("p q h -> p (q h)"), ct("ident16")))
                parts_ready = act.did(act.after(turned).activation(
                    cum_parts[:, 8 * P * k:8 * P * k + 8 * P], psum[:, 4 + k, :].bitcast(BF16)[0:3 * NH, :], ACT.Copy))

            m = pool.did(pool.after(dt_ready).tensor_tensor(
                freq_dt.rearrange("p (j f) -> p j f", f=HALF), dt.unsqueeze(2).to_broadcast([P, n4, HALF]),
                wt("inv_freq").unsqueeze(1).to_broadcast([P, n4, HALF]), ALU.mult))
            pe.after(m)
            cos_cols, sin_cols = products[0], None
            angle_ring = Ring([psum[:, i, :] for i in (6, 7)])
            turned_marks = []
            rounds = [products[i] for i in range(4)]
            reduced_free = [None, None]
            for g in range(NGRP):
                bank, free = angle_ring.take()
                pe.after(free)
                for s in range(2):
                    j = GB * g + 2 * s
                    cols = bank[:, SEQ * s:SEQ * s + SEQ]
                    nc.tensor.matmul(cols, freq_dt[:, P * j:P * j + P], tri, start=(s == 0), stop=True, skip_group_check=True)
                    angles = pe.did(nc.tensor.matmul(cols[:, P:SEQ], freq_dt[:, P * j + P:P * j + 2 * P], tri[:, 0:P],
                                                     start=False, stop=True, skip_group_check=True))
                a, b = rounds[0], rounds[1]
                ns, ncos = sine[:, BANK * g:BANK * g + BANK], cosine[:, BANK * g:BANK * g + BANK]
                dve.after(angles)
                m1 = dve.did(nc.vector.tensor_scalar(a, bank, ROUND, None, ALU.add))
                m2 = dve.did(nc.vector.tensor_scalar(b, bank, 0.25, ROUND, ALU.add, ALU.add))
                m1 = dve.did(dve.after(m1).scalar_tensor_tensor(ns, a, ROUND, bank, ALU.subtract, ALU.subtract))
                m2 = dve.did(dve.after(m2).scalar_tensor_tensor(ncos, b, ROUND, bank, ALU.subtract, ALU.subtract))
                dve.after(m2)
                angle_ring.release(bank, m2)
                turned_marks.append(m2)
            act.after(turned_marks[-1])
            full_turn = 6.283185
            trig = []
            for g in range(NGRP):
                cols = slice(BANK * g, BANK * g + BANK)
                nc.scalar.activation(sine[:, cols], sine[:, cols], ACT.Sin, scale=-full_turn)
                trig.append(act.did(nc.scalar.activation(cosine[:, cols], cosine[:, cols], ACT.Sin, scale=-full_turn,
                                                         bias=quarter_turn)))

            ring = Ring([psum[:, i, :] for i in range(8)])
            pe.after(parts_ready, turned_marks[-1])
            for g in range(NGRP):
                for c in range(NPAIR):
                    bank, free = ring.take()
                    z_ready = pe.did(pe.after(free).matmul(bank, z_w[:, P * c:P * c + P], xnt_group(g), start=True, stop=True))
                    ring.release(bank, act.did(act.after(z_ready).activation(z_silu[:, c, BANK * g:BANK * g + BANK], bank, ACT.Silu)))
            product_free = [m2] * 8
            rotated_ready = []
            for g in range(NGRP):
                cols = slice(BANK * g, BANK * g + BANK)
                for k in range(2):
                    p0, p1, p2, p3 = products[4 * k:4 * k + 4]
                    bank0, free0 = ring.take()
                    bank1, free1 = ring.take()
                    r0 = pe.did(pe.after(free0).matmul(bank0, bc_w[:, 2 * P * k:2 * P * k + P], xnt_group(g), start=True, stop=True))
                    r1 = pe.did(pe.after(free1).matmul(bank1, bc_w[:, 2 * P * k + P:2 * P * k + 2 * P], xnt_group(g),
                                                       start=True, stop=True))
                    dve.after(r0, trig[g], product_free[k])
                    nc.vector.tensor_tensor(p0, bank0, cosine[:, cols], ALU.mult)
                    m = dve.did(nc.vector.tensor_tensor(p2, bank0, sine[:, cols], ALU.mult))
                    ring.release(bank0, m)
                    dve.after(r1)
                    m0 = dve.did(nc.vector.tensor_tensor(p1, bank1, sine[:, cols], ALU.mult))
                    m1 = dve.did(nc.vector.tensor_tensor(p3, bank1, cosine[:, cols], ALU.mult))
                    ring.release(bank1, m1)
                    pool.after(m1)
                    nc.gpsimd.tensor_tensor(rotated[k][0][:, cols], p0, p1, ALU.subtract)
                    product_free[k] = pool.did(nc.gpsimd.tensor_tensor(rotated[k][1][:, cols], p2, p3, ALU.add))
                    rotated_ready.append(product_free[k])
            for j in range(0, NBLK, 2):
                bank, free = ring.take()
                pe.after(free)
                for i in range(2):
                    r = pe.did(nc.tensor.matmul(bank[:, 2 * P * i:2 * P * i + 2 * P], xnt_block(j + i), xr_w, start=True, stop=True))
                dve.after(r, turned_marks[-1], weight_ready)
                xw_ready = dve.did(nc.vector.tensor_tensor(
                    xw[:, j:j + 2, :, :].rearrange("p j h c -> p (j h) c"), bank.rearrange("p (q c) -> p q c", c=HD),
                    v[:, NH * j:NH * j + 2 * NH].unsqueeze(2).to_broadcast([P, 2 * NH, HD]), ALU.mult))
                ring.release(bank, xw_ready)

            next_layer()
            exponents = Ring([psum[:, i, :] for i in range(3)])
            scores = Ring([psum[:, i, :] for i in range(3, 6)])
            outputs = Ring([psum[:, i, :] for i in range(6, 8)])
            z_gated = [None] * BATCH
            mixed_free, decay_free = [None] * 3, [None] * 3
            units = [(b, h) for b in range(BATCH) for h in range(NH)]
            pending = []

            def attend(i, b, h):
                rows = slice(HALF * h, HALF * h + HALF)
                t0, tm, t1 = SEQ * b, SEQ * b + P, SEQ * b + SEQ
                bank, free = exponents.take()
                pe.after(free)
                pick = ct("pick_head", slice(0, 3 * NH))[:, P * h:P * h + P]
                nc.tensor.matmul(bank[:, 0:2 * P], pick, cum_parts[:, t0:t1], start=True, stop=True, skip_group_check=True)
                nc.tensor.matmul(bank[:, 2 * P:3 * P], pick, cum_parts[:, tm:t1], start=False, stop=True, skip_group_check=True)
                exponent = pe.did(nc.tensor.matmul(bank[:, 0:3 * P], ct("ident16"), ct("mask16"), start=False, stop=True,
                                                   skip_group_check=True))
                d = decay[i % 3]
                act.after(exponent, decay_free[i % 3])
                j = 2 * b
                nc.scalar.activation(d[:, 0:2 * P], bank[:, 0:2 * P], ACT.Exp, bias=neg_cum[:, NH * j + h:NH * j + h + 1])
                decayed = act.did(nc.scalar.activation(d[:, 2 * P:3 * P], bank[:, 2 * P:3 * P], ACT.Exp,
                                                       bias=neg_cum[:, NH * (j + 1) + h:NH * (j + 1) + h + 1]))
                exponents.release(bank, decayed)
                dve.after(decayed)
                for k, cols in ((0, slice(0, P)), (1, slice(2 * P, 3 * P))):
                    fixed = dve.did(nc.vector.scalar_tensor_tensor(
                        d[:, cols], ident, neg_u[:, NH * (j + k) + h:NH * (j + k) + h + 1], d[:, cols], ALU.mult, ALU.add))
                bank, free = scores.take()
                pe.after(free)
                for k in range(2):
                    b_rows, c_rows = rotated[0][k][rows, :], rotated[1][k][rows, :]
                    nc.tensor.matmul(bank[:, 0:2 * P], b_rows[:, t0:tm], c_rows[:, t0:t1], start=(k == 0), stop=(k == 1),
                                     skip_group_check=True)
                for k in range(2):
                    b_rows, c_rows = rotated[0][k][rows, :], rotated[1][k][rows, :]
                    scored = nc.tensor.matmul(bank[:, 2 * P:3 * P], b_rows[:, tm:t1], c_rows[:, tm:t1], start=False,
                                              stop=(k == 1), skip_group_check=True)
                scored = pe.did(scored)
                dve.after(scored, fixed, mixed_free[i % 3])
                m = dve.did(nc.vector.tensor_tensor(mixed[i % 3], bank[:, 0:3 * P], d, ALU.mult))
                scores.release(bank, m)
                decay_free[i % 3] = m
                return m

            y_bank = [None, None]

            def emit(i, b, h, mixed_ready):
                if h == 0:
                    y_bank[0], y_bank[1] = outputs.take()
                bank = y_bank[0]
                pe.after(mixed_ready, y_bank[1])
                rows, at = slice(HD * (h % 2), HD * (h % 2) + HD), SEQ * (h // 2)
                g = mixed[i % 3]
                nc.tensor.matmul(bank[rows, at:at + SEQ], xw[:, 2 * b, h, :], g[:, 0:2 * P], start=True, stop=True,
                                 skip_group_check=True)
                m = pe.did(nc.tensor.matmul(bank[rows, at + P:at + SEQ], xw[:, 2 * b + 1, h, :], g[:, 2 * P:3 * P],
                                            start=False, stop=True, skip_group_check=True))
                mixed_free[i % 3] = m
                if h == NH - 1:
                    gate = z_silu[:, :, SEQ * b:SEQ * b + SEQ]
                    z_gated[b] = dve.did(dve.after(m).tensor_tensor(
                        gate, bank.rearrange("p (c t) -> p c t", c=NPAIR), gate, ALU.mult))
                    outputs.release(bank, z_gated[b])

            for i, (b, h) in enumerate(units):
                pending.append((i, b, h, attend(i, b, h)))
                if len(pending) == 2:
                    emit(*pending.pop(0))
            emit(*pending.pop(0))

            for c in range(NPAIR):
                w_ready = dve.did(nc.vector.tensor_scalar(out_w[:, DM * c:DM * c + DM], wt("out_a")[:, DM * c:DM * c + DM],
                                                          wt("norm_w")[:, c:c + 1], None, ALU.mult))
            next_layer()
            squares = xw.rearrange("p j h c -> p (j h c)").rearrange("p (c t) -> p c t", c=NPAIR)
            sum_bank = psum[:, 0, 0:NBLK]
            for b in range(BATCH):
                cols = slice(SEQ * b, SEQ * b + SEQ)
                m = act.did(nc.scalar.activation(squares[:, :, cols], z_silu[:, :, cols], ACT.Square))
                pe.after(m)
                for j in (2 * b, 2 * b + 1):
                    for c in range(NPAIR):
                        s = nc.tensor.matmul(sum_bank[:, j:j + 1], squares[:, c, P * j:P * j + P], tri[:, P:P + 1],
                                             start=(c == 0), stop=(c == NPAIR - 1))
            summed = pe.did(s)
            root = act.did(act.after(summed).activation(deviation[:], sum_bank, ACT.Sqrt, bias=eps_rms, scale=1.0 / (NH * HD)))
            scale_ready = dve.did(dve.after(root).reciprocal(rstd[:], deviation[:]))
            ring = Ring([psum[:, i, :] for i in range(1, 8)])
            dve.after(scale_ready)
            for g in range(NGRP):
                bank, free = ring.take()
                pe.after(free)
                for q in range(GB):
                    j = GB * g + q
                    for c in range(NPAIR):
                        r = nc.tensor.matmul(bank[:, P * q:P * q + P], z_silu[:, c, P * j:P * j + P],
                                             out_w[:, DM * c:DM * c + DM], start=(c == 0), stop=(c == NPAIR - 1))
                r = pe.did(r)
                dve.after(r)
                for q in range(GB):
                    j = GB * g + q
                    added = dve.did(nc.vector.scalar_tensor_tensor(x[:, j, :], bank[:, P * q:P * q + P], rstd[:, j:j + 1],
                                                                   x[:, j, :], ALU.mult, ALU.add))
                ring.release(bank, added)
            return added

        def experts(turn, x_ready):
            piece = carve()
            xs_rows = piece(NSLOT * DM).rearrange("p (s c) -> p s c", s=NSLOT)
            xs_t = piece(NSLOT * P)
            y_rows = piece(NSLOT * DM).rearrange("p (s c) -> p s c", s=NSLOT)
            scaled = piece(NBLK * DM).rearrange("p (j c) -> p j c", j=NBLK)
            gathered = piece(NBLK * DM).rearrange("p (j c) -> p j c", j=NBLK)
            shared_act = [piece(NSC * BANK).rearrange("p (c t) -> p c t", c=NSC) for _ in range(2)]
            shared_gate = [piece(BANK) for _ in range(2)]
            gate = [piece(2 * EF) for _ in range(2)]
            hidden = [piece(2 * EF) for _ in range(2)]
            hidden_t = [piece(2 * EF) for _ in range(2)]
            logit_max, best, score, position = (piece(NBLK) for _ in range(4))
            position_int = piece(NBLK).bitcast(I32)
            chosen, one_hot, totals, running, base, rank = (piece(NBLK * NE) for _ in range(6))
            one_hot16 = piece(NBLK * NE // 2).bitcast(BF16)
            n_slots, end_slot, start_row = (piece(NE) for _ in range(3))
            passed = piece(NSLOT * NE)
            expert = piece(NSLOT)
            expert_int = piece(NSLOT).bitcast(I32)

            normed = normalise(x_ready)

            def by_token(t):
                return t.rearrange("p (j n) -> p j n", n=NE)

            def by_expert(t):
                return t.rearrange("p (n j) -> p j n", j=NBLK)

            logits = psum[:, 2, 0:NBLK * NE]
            pe.after(normed)
            for j in range(NBLK):
                r = nc.tensor.matmul(logits[:, NE * j:NE * j + NE], xnt_block(j), wt("router"), start=True, stop=True)
            r = pe.did(r)
            m_max = dve.did(dve.after(r).tensor_reduce(logit_max, by_token(logits), AX.X, ALU.max))
            m = dve.did(dve.after(m_max).tensor_tensor(
                by_token(chosen), by_token(logits), logit_max.unsqueeze(2).to_broadcast([P, NBLK, NE]), ALU.is_equal))
            rev = wt("rev_expert").unsqueeze(1).to_broadcast([P, NBLK, NE])
            m = dve.did(dve.after(m).tensor_tensor(by_token(rank), by_token(chosen), rev, ALU.mult))
            m = dve.did(dve.after(m).tensor_reduce(best, by_token(rank), AX.X, ALU.max))
            m_hot = dve.did(dve.after(m).tensor_tensor(
                by_token(one_hot), rev, best.unsqueeze(2).to_broadcast([P, NBLK, NE]), ALU.is_equal))
            m_hot16 = dve.did(dve.after(m_hot).tensor_copy(one_hot16, one_hot))
            scored = act.did(act.after(m_max).activation(score, logit_max, ACT.Sigmoid))
            pe.after(m_hot16)
            in_block, block_total = psum[:, 3, 0:NBLK * NE], psum[:, 4, 0:NBLK * NE]
            nc.tensor.matmul(in_block, ct("tri16"), one_hot16, start=True, stop=True)
            r = pe.did(nc.tensor.matmul(block_total, ct("ones16"), one_hot16, start=True, stop=True))
            scaled_ready = dve.did(dve.after(scored).tensor_tensor(
                scaled, xn[:], score.unsqueeze(2).to_broadcast([P, NBLK, DM]), ALU.mult))
            m = dve.did(dve.after(r).tensor_copy(by_expert(totals), by_token(block_total)))
            m_run = dve.did(dve.after(m).tensor_tensor_scan(running, wt("keep"), totals, 0.0, ALU.mult, ALU.add))
            counts = running.rearrange("p (n j) -> p n j", j=NBLK)[:, :, NBLK - 1]
            m = dve.did(dve.after(m_run).tensor_scalar(n_slots, counts, 1.0 / P, (P - 1.0) / P - (P - 1.0) / (2 * P), ALU.mult, ALU.add))
            m = dve.did(dve.after(m).tensor_scalar(n_slots, n_slots, ROUND, -ROUND, ALU.add, ALU.add))
            m_end = dve.did(dve.after(m).tensor_tensor_scan(end_slot, tri[:, P:P + NE], n_slots, 0.0, ALU.mult, ALU.add))
            m = dve.did(dve.after(m_end).tensor_tensor(start_row, end_slot, n_slots, ALU.subtract))
            m = dve.did(dve.after(m).tensor_scalar(start_row, start_row, float(P), -1.0, ALU.mult, ALU.add))
            m = dve.did(dve.after(m).tensor_tensor(base, running, totals, ALU.subtract))
            m = dve.did(dve.after(m).tensor_tensor(base.rearrange("p (n j) -> p n j", j=NBLK), base.rearrange("p (n j) -> p n j", j=NBLK),
                                                   start_row.unsqueeze(2).to_broadcast([P, NE, NBLK]), ALU.add))
            m = dve.did(dve.after(m).tensor_tensor(by_token(rank), by_token(in_block), by_expert(base), ALU.add))
            m = dve.did(dve.after(m).tensor_tensor(rank, rank, one_hot, ALU.mult))
            m = dve.did(dve.after(m).tensor_reduce(position, by_token(rank), AX.X, ALU.add))
            placed = dve.did(dve.after(m).tensor_copy(position_int, position))
            m = dve.did(dve.after(m_end).tensor_tensor(
                passed.rearrange("p (s n) -> p s n", n=NE), wt("slot").unsqueeze(2).to_broadcast([P, NSLOT, NE]),
                end_slot.unsqueeze(1).to_broadcast([P, NSLOT, NE]), ALU.is_ge))
            m = dve.did(dve.after(m).tensor_reduce(expert, passed.rearrange("p (s n) -> p s n", n=NE), AX.X, ALU.add))
            m = dve.did(dve.after(m).tensor_scalar(expert, expert, float(NE - 1), None, ALU.min))
            expert_ready = dve.did(dve.after(m).tensor_copy(expert_int, expert))

            scatter, fetch = Transfers(sem(f"scatter{turn}")), Transfers(sem(f"fetch{turn}"))
            store, gather = Transfers(sem(f"store{turn}")), Transfers(sem(f"gather{turn}"))
            pool.after(placed, scaled_ready, zero_fill.last())
            for j in range(NBLK):
                scatter.sent(nc.gpsimd.indirect_dma_start(
                    sorted_x[turn], bass.IndirectOffsetOnAxis(position_int[:, j:j + 1], 0), scaled[:, j, :], None))
            fetch.sent(sp.after(scatter.last()).dma_start(xs_rows, sorted_x[turn].rearrange("(s p) c -> p s c", p=P)))

            up_ring = Ring([psum[:, i, :] for i in (5, 6)])
            gate_ring = Ring([psum[:, i, :] for i in (7, 0)])
            down_ring = Ring([psum[:, i, :] for i in (1, 2)])
            pe.after(placed)
            shared_added = [None] * NGRP
            down_done = [None] * NGRP
            gate_free = [None, None]

            def shared_down(g):
                bank, free = down_ring.take()
                pe.after(free, hidden_ready[g])
                for q in range(GB):
                    for c in range(NSC):
                        r = nc.tensor.matmul(bank[:, P * q:P * q + P], shared_act[g % 2][:, c, P * q:P * q + P],
                                             wt("shared_down")[:, DM * c:DM * c + DM], start=(c == 0), stop=(c == NSC - 1))
                down_done[g] = pe.did(r)
                cols = x_cols[:, BANK * g:BANK * g + BANK]
                shared_added[g] = dve.did(dve.after(down_done[g]).tensor_tensor(cols, bank, cols, ALU.add))
                down_ring.release(bank, shared_added[g])

            hidden_ready = [None] * NGRP
            for g in range(NGRP):
                for c in range(NSC):
                    cols = slice(P * c, P * c + P)
                    bank_g, free = gate_ring.take()
                    r = pe.did(pe.after(free).matmul(bank_g, wt("shared_gate")[:, cols], xnt_group(g), start=True, stop=True))
                    sg = shared_gate[c % 2]
                    m = act.did(act.after(r, gate_free[c % 2]).activation(sg, bank_g, ACT.Silu))
                    gate_ring.release(bank_g, m)
                    bank_u, free = up_ring.take()
                    r = pe.did(pe.after(free).matmul(bank_u, wt("shared_up")[:, cols], xnt_group(g), start=True, stop=True))
                    dve.after(r, m, down_done[g - 2] if g >= 2 else None)
                    hidden_ready[g] = dve.did(nc.vector.tensor_tensor(shared_act[g % 2][:, c, :], bank_u, sg, ALU.mult))
                    gate_free[c % 2] = hidden_ready[g]
                    up_ring.release(bank_u, hidden_ready[g])
                if g >= 1:
                    shared_down(g - 1)
            shared_down(NGRP - 1)

            next_layer(fetch.last())
            turn_ring = Ring([psum[:, i, :] for i in (0, 1)])
            turned_in = [None] * NSLOT
            for s0 in range(0, NSLOT, GB):
                n = min(GB, NSLOT - s0)
                bank, free = turn_ring.take()
                pe.after(free)
                for q in range(n):
                    r = nc.tensor.transpose(bank[:, P * q:P * q + P], xs_rows[:, s0 + q, :], ident)
                r = pe.did(r)
                m = act.did(act.after(r).activation(xs_t[:, P * s0:P * s0 + P * n], bank[:, 0:P * n], ACT.Copy))
                turn_ring.release(bank, m)
                for q in range(n):
                    turned_in[s0 + q] = m
            up_ring = Ring([psum[:, i, :] for i in (2, 3)])
            flip_ring = Ring([psum[:, i, :] for i in (4, 5)])
            down_ring = Ring([psum[:, i, :] for i in (6, 7)])
            pairs = [tuple(range(s, min(s + 2, NSLOT))) for s in range(0, NSLOT, 2)]
            chosen_expert = {}
            gate_up, down = wt("gate_up"), wt("down")
            hidden_free, flipped_free, gate_used = [None] * 2, [None] * 2, [None] * 2
            stage1, stage2 = {}, {}

            def expand(k):
                bank, free = up_ring.take()
                pe.after(free, [turned_in[s] for s in pairs[k]], expert_ready)
                for q, s in enumerate(pairs[k]):
                    chosen_expert[s] = nc.tensor.value_load(expert_int[0:1, s:s + 1], min_val=0, max_val=NE - 1)
                    r = nc.tensor.matmul(bank[:, 2 * EF * q:2 * EF * q + 2 * EF], xs_t[:, P * s:P * s + P],
                                         gate_up[:, bass.ds(chosen_expert[s] * (2 * EF), 2 * EF)], start=True, stop=True)
                r = pe.did(r)
                n = len(pairs[k])
                halves = bank.rearrange("p (q u f) -> p q u f", q=2, u=2)
                gt = gate[k % 2].rearrange("p (q f) -> p q f", q=2)[:, 0:n, :]
                m = act.did(act.after(r, gate_used[k % 2]).activation(gt, halves[:, 0:n, 0, :], ACT.Silu))
                hd = hidden[k % 2].rearrange("p (q f) -> p q f", q=2)[:, 0:n, :]
                m = dve.did(dve.after(m, hidden_free[k % 2]).tensor_tensor(hd, halves[:, 0:n, 1, :], gt, ALU.mult))
                gate_used[k % 2] = m
                up_ring.release(bank, m)
                stage1[k] = m

            def flip(k):
                bank, free = flip_ring.take()
                pe.after(free, stage1[k])
                n = len(pairs[k])
                for q in range(n):
                    r = nc.tensor.transpose(bank[:, P * q:P * q + P], hidden[k % 2][:, EF * q:EF * q + EF], ident)
                r = pe.did(r)
                hidden_free[k % 2] = r
                m = dve.did(dve.after(r, flipped_free[k % 2]).tensor_copy(hidden_t[k % 2][:, 0:P * n], bank[:, 0:P * n]))
                flip_ring.release(bank, m)
                stage2[k] = m

            stored = []

            def contract(k):
                bank, free = down_ring.take()
                pe.after(free, stage2[k])
                for q, s in enumerate(pairs[k]):
                    r = nc.tensor.matmul(bank[:, P * q:P * q + P], hidden_t[k % 2][:, P * q:P * q + P],
                                         down[:, bass.ds(chosen_expert[s] * DM, DM)], start=True, stop=True)
                r = pe.did(r)
                flipped_free[k % 2] = r
                n = len(pairs[k])
                s0 = pairs[k][0]
                m = act.did(act.after(r).activation(y_rows[:, s0:s0 + n, :], bank[:, 0:P * n].rearrange("p (q c) -> p q c", q=n), ACT.Copy))
                down_ring.release(bank, m)
                rows = sorted_y[turn].rearrange("(s p) c -> p s c", p=P)
                if k % 4 == 3 or k == len(pairs) - 1:
                    first = pairs[k - k % 4][0]
                    store.sent(sp.after(m).dma_start(rows[:, first:s0 + n, :], y_rows[:, first:s0 + n, :]))

            for k in range(len(pairs) + 2):
                if k < len(pairs):
                    expand(k)
                if 1 <= k <= len(pairs):
                    flip(k - 1)
                if k >= 2:
                    contract(k - 2)
            pool.after(store.last())
            for j in range(NBLK):
                gather.sent(nc.gpsimd.indirect_dma_start(
                    gathered[:, j, :], None, sorted_y[turn], bass.IndirectOffsetOnAxis(position_int[:, j:j + 1], 0)))
            added = dve.did(dve.after(gather.last(), shared_added).tensor_tensor(x[:], x[:], gathered, ALU.add))
            return added

        def selective_scan(x_ready):
            piece = carve()
            u = piece(NCH * NTOK).rearrange("p (c t) -> p c t", c=NCH)
            z = piece(NCH * NTOK).rearrange("p (c t) -> p c t", c=NCH)
            dt = piece(NCH * NTOK).rearrange("p (c t) -> p c t", c=NCH)
            dtu = piece(NCH * NTOK).rearrange("p (c t) -> p c t", c=NCH)
            u_w = piece(DC * DI)
            a_neg = piece(NCH * DS)
            work = [piece(BANK) for _ in range(4)]
            low = piece(BANK * NGRP, slice(0, 2 * DS + DR))
            rest = piece(BANK, slice(0, 2 * DS))
            high16, mid16 = (piece(BANK // 2, slice(0, 2 * DS)).bitcast(BF16) for _ in range(2))
            rows16 = piece(NTOK // 2, slice(0, 6 * DS)).bitcast(BF16)
            n_decay = 2
            step = 1024
            gates = [dt, dtu]
            free_space = piece(0)
            decay = [xn[:].rearrange("p j c -> p (j c)")[:, i * HTOK:(i + 1) * HTOK] for i in range(2)]
            driven = [piece(HTOK) for _ in range(2)]
            state = [piece(HTOK) for _ in range(2)]

            conv_w, in_b = wt("conv_w"), wt("in_b")
            dve.after(load_late.last())
            for k in range(DC):
                w_ready = dve.did(nc.vector.tensor_tensor(u_w[:, DI * k:DI * k + DI], in_b[:, 0:DI], conv_w[:, DI * k:DI * k + DI],
                                                          ALU.mult))
            a_exp = act.did(act.after(load_late.last()).activation(a_neg, wt("a_log_b"), ACT.Exp))
            a_ready = dve.did(dve.after(a_exp).tensor_scalar(a_neg, a_neg, -1.0, None, ALU.mult))
            normed = normalise(x_ready)
            next_layer()
            ring = Ring([psum[:, i, :] for i in range(8)])
            u_ready = [[None] * NCH for _ in range(NGRP)]
            for g in range(NGRP):
                cols = slice(BANK * g, BANK * g + BANK)
                for c in range(NCH):
                    bank, free = ring.take()
                    pe.after(free)
                    for k in range(DC):
                        r = nc.tensor.matmul(bank, u_w[:, DI * k + P * c:DI * k + P * c + P], xnt[:, 2 * g:2 * g + 2, k:k + SEQ],
                                             start=(k == 0), stop=(k == DC - 1))
                    r = pe.did(r)
                    u_ready[g][c] = act.did(act.after(r).activation(u[:, c, cols], bank, ACT.Silu, bias=wt("conv_b")[:, c:c + 1]))
                    ring.release(bank, u_ready[g][c])
                    bank, free = ring.take()
                    r = pe.did(pe.after(free).matmul(bank, in_b[:, DI + P * c:DI + P * c + P], xnt_group(g), start=True, stop=True))
                    m = act.did(act.after(r).activation(z[:, c, cols], bank, ACT.Silu))
                    ring.release(bank, m)
            rows_free = None
            for g in range(NGRP):
                cols = slice(BANK * g, BANK * g + BANK)
                bank, free = ring.take()
                pe.after(free, u_ready[g])
                nr = 2 * DS + DR
                for c in range(NCH):
                    r = nc.tensor.matmul(bank[0:nr, :], wt("x_b")[:, nr * c:nr * c + nr], u[:, c, cols], start=(c == 0), stop=(c == NCH - 1))
                r = pe.did(r)
                low_ready = act.did(act.after(r).activation(low[:, cols], bank[0:nr, :], ACT.Copy))
                ring.release(bank, low_ready)
                lo = low[0:2 * DS, cols]
                dve.after(low_ready)
                m = dve.did(nc.vector.tensor_copy(high16, lo))
                m = dve.did(dve.after(m).tensor_tensor(rest, lo, high16, ALU.subtract))
                m = dve.did(dve.after(m).tensor_copy(mid16, rest))
                dve.after(m)
                nc.vector.tensor_copy(rows16[0:2 * DS, cols], high16)
                nc.vector.tensor_copy(rows16[2 * DS:4 * DS, cols], mid16)
                rows_ready = dve.did(nc.vector.tensor_tensor(rows16[4 * DS:6 * DS, cols], rest, mid16, ALU.subtract))
                dve.after(rows_ready)
                for c in range(NCH):
                    bank, free = ring.take()
                    r = pe.did(pe.after(free, low_ready).matmul(
                        bank, wt("dt_w", slice(2 * DS, nr))[:, P * c:P * c + P], low[2 * DS:nr, cols], start=True, stop=True))
                    act.after(r, rows_free)
                    m = act.did(nc.scalar.activation(work[0], bank, ACT.Abs, bias=wt("dt_b")[:, c:c + 1]))
                    m_relu = act.did(nc.scalar.activation(work[1], bank, ACT.Relu, bias=wt("dt_b")[:, c:c + 1]))
                    ring.release(bank, m_relu)
                    m = act.did(act.after(m).activation(work[2], work[0], ACT.Exp, scale=-1.0))
                    m = act.did(act.after(m).activation(work[3], work[2], ACT.Ln, bias=one))
                    rows_free = dve.did(dve.after(m, m_relu).tensor_tensor(dt[:, c, cols], work[1], work[3], ALU.add))
                    dtu_ready = pool.did(pool.after(rows_free, u_ready[g][c]).tensor_tensor(dtu[:, c, cols], dt[:, c, cols], u[:, c, cols], ALU.mult))

            for i in range(2):
                starts = decay[i].rearrange("p (s t) -> p s t", t=SEQ)[:, :, 0:1]
                starts_zero = dve.did(nc.vector.memset(starts, 0.0))
            next_layer()
            b_bank, c_bank = psum[:, 0:2, :], psum[:, 2:4, :]
            b_free = c_free = None
            decay_free, state_free = [None] * 2, [None] * 2
            y_free = [None] * NCH
            nseq = BATCH // 2

            def flat(banks):
                return banks.rearrange("p b t -> p (b t)")

            pick_row = ct("pick_row", slice(0, 6 * DS))
            for half in range(2):
                t0 = HTOK * half
                cols = slice(t0, t0 + HTOK)
                y_banks = [psum[:, 4 + 2 * c:6 + 2 * c, :] for c in range(NCH)]
                added_c = [None] * NCH
                for n in range(DS):
                    for row, banks, free in ((n, b_bank, b_free), (DS + n, c_bank, c_free)):
                        pe.after(free)
                        for i in range(2):
                            r = nc.tensor.matmul(banks[:, i, :], pick_row[:, P * row:P * row + P],
                                                 rows16[:, t0 + BANK * i:t0 + BANK * i + BANK], start=True, stop=True)
                        r = pe.did(r)
                        if row == n:
                            b_ready = r
                        else:
                            c_ready = r
                    for c in range(NCH):
                        live = decay[c].rearrange("p (s t) -> p s t", t=SEQ)[:, :, 1:SEQ]
                        seq = dt[:, c, cols].rearrange("p (s t) -> p s t", t=SEQ)[:, :, 1:SEQ]
                        act.after(decay_free[c])
                        d_ready = act.did(nc.scalar.activation(live, seq, ACT.Exp, scale=a_neg[:, DS * c + n:DS * c + n + 1]))
                        b_used = dve.did(dve.after(b_ready).tensor_tensor(driven[c], dtu[:, c, cols], flat(b_bank), ALU.mult))
                        if c == 0:
                            first_driven, first_decay = b_used, d_ready
                    b_free = b_used
                    for c, marks in ((0, [first_driven, first_decay]), (1, [b_used, d_ready])):
                        dve.after(marks, state_free[c])
                        scanned = dve.did(nc.vector.tensor_tensor_scan(state[c], decay[c], driven[c], 0.0, ALU.mult, ALU.add))
                        decay_free[c] = scanned
                        if c == 0:
                            first_scanned = scanned
                    for c, mark in ((0, first_scanned), (1, scanned)):
                        m = dve.did(dve.after(mark, c_ready).tensor_tensor(state[c], state[c], flat(c_bank), ALU.mult))
                        pe.after(m, y_free[c])
                        for i in range(2):
                            r = nc.tensor.matmul(y_banks[c][:, i, :], ident, state[c][:, BANK * i:BANK * i + BANK],
                                                 start=(n == 0), stop=(n == DS - 1))
                        state_free[c] = pe.did(r)
                    c_free = m
                for c in range(NCH):
                    m = dve.did(dve.after(state_free[c]).scalar_tensor_tensor(
                        u[:, c, cols], u[:, c, cols], wt("d_b")[:, c:c + 1], flat(y_banks[c]), ALU.mult, ALU.add))
                    y_free[c] = m
                    y_ready = dve.did(dve.after(m).tensor_tensor(z[:, c, cols], z[:, c, cols], u[:, c, cols], ALU.mult))
            next_layer()
            ring = Ring([psum[:, i, :] for i in range(8)])
            for g in range(NGRP):
                bank, free = ring.take()
                pe.after(free)
                for q in range(GB):
                    j = GB * g + q
                    for c in range(NCH):
                        r = nc.tensor.matmul(bank[:, P * q:P * q + P], z[:, c, P * j:P * j + P], wt("out_b")[:, DM * c:DM * c + DM],
                                             start=(c == 0), stop=(c == NCH - 1))
                r = pe.did(r)
                xc = x_cols[:, BANK * g:BANK * g + BANK]
                added = dve.did(dve.after(r).tensor_tensor(xc, xc, bank, ALU.add))
                ring.release(bank, added)
            return added

        x_ready = state_space()
        next_layer(load_late.last(), zero_fill.last())
        x_ready = experts(0, x_ready)
        next_layer()
        x_ready = selective_scan(x_ready)
        next_layer()
        x_ready = experts(1, x_ready)
        written = Transfers(sem("written"))
        written.sent(sp.after(x_ready).dma_start(out, x_cols))
        sp.after(written.last())


def constants():
    k, m = np.arange(P)[:, None], np.arange(P)[None, :]
    f = {
        "ident": k == m,
        "tri": np.concatenate([k <= m, np.ones((P, P))], 1),
        "shift": k == m + 1,
        "shift_in": (k == 0) & (m == P - 1),
        "inv_freq": (1.0 / 10000.0 ** (np.arange(HALF) / HALF) / (2 * np.pi))[None, :],
        "rev_expert": (NE - np.arange(NE))[None, :],
        "keep": np.tile(np.arange(NBLK) != 0, NE)[None, :],
        "slot": np.arange(NSLOT)[None, :],
    }
    row = np.arange(P)[:, None]
    mask = np.where(m < k, MASKED, 0.0)
    h = {
        "ident16": k == m,
        "tri16": k <= m,
        "ones16": np.ones((P, P)),
        "mask16": np.concatenate([mask, np.zeros((P, P)), mask], 1),
        "pick_head": (row < 3 * NH) & (row % NH == np.repeat(np.arange(NH), P)[None, :]),
        "pick_row": (row < 6 * DS) & (row % (2 * DS) == np.repeat(np.arange(2 * DS), P)[None, :]),
    }
    c16 = np.zeros((P, C_COLS), np.uint16)
    for name, value in h.items():
        at, width = C_AT[name]
        c16[:, at:at + width] = np.broadcast_to(value, (P, width)).astype(np.float32).view(np.uint32) >> 16
    return f, c16


def kernel(**inputs):
    import numpy as _np
    import concourse.bacc as _bacc
    from concourse import mybir as _mybir
    from concourse.bass_utils import run_bass_kernel_spmd as _run

    i = {name: _np.asarray(a) for name, a in inputs.items()}
    f32_consts, c16 = constants()

    def halves(a):
        return a.reshape(-1, P, a.shape[-1]).transpose(1, 0, 2).reshape(P, -1)

    wa = i["L0_attn_a_W_in"]
    z, xr, bm, cm, dtc = _np.split(wa, [256, 512, 768, 1024], axis=1)
    nr = 2 * DS + DR
    wx = _np.concatenate([i["L0_attn_b_W_x"][DR:nr], i["L0_attn_b_W_x"][0:DR]], 0).T
    packed = {
        "in_a": _np.concatenate([z, bm[:, 0::2], bm[:, 1::2], cm[:, 0::2], cm[:, 1::2], xr, dtc], 1),
        "dt_bias": i["L0_attn_a_dt_bias"][None, :],
        "a_log_a": i["L0_attn_a_A_log"][None, :],
        "norm_w": i["L0_attn_a_norm_weight"].reshape(NPAIR, P).T,
        "out_a": halves(i["L0_attn_a_W_out"]),
        "router": i["L0_ffn_router_w"].T,
        "shared_gate": i["L0_ffn_shared_gate_w"].T,
        "shared_up": i["L0_ffn_shared_up_w"].T,
        "shared_down": halves(i["L0_ffn_shared_down_w"].T),
        "gate_up": i["L0_ffn_gate_up_proj"].transpose(1, 0, 2).reshape(P, -1),
        "down": i["L0_ffn_down_proj"].transpose(1, 0, 2).reshape(P, -1),
        "in_b": i["L0_attn_b_W_in"].T,
        "conv_w": i["L0_attn_b_conv_w"].T.reshape(1, -1),
        "conv_b": i["L0_attn_b_conv_b"].reshape(NCH, P).T,
        "x_b": halves(wx),
        "dt_b": i["L0_attn_b_b_dt"].reshape(NCH, P).T,
        "a_log_b": halves(i["L0_attn_b_A_log"]),
        "d_b": i["L0_attn_b_D"].reshape(NCH, P).T,
        "out_b": halves(i["L0_attn_b_W_out"].T),
    }
    packed.update(f32_consts)
    w = _np.zeros((P, W_COLS), _np.float32)
    for name, value in packed.items():
        at, width = W_AT[name]
        w[:, at:at + width] = value
    at, width = W_AT["dt_w"]
    w[2 * DS:nr, at:at + width] = i["L0_attn_b_W_dt"].T
    x = i["L0_attn_a_hidden"].reshape(NBLK, P, DM).transpose(1, 0, 2).reshape(P, NBLK * DM)
    arrays = {"x_in": _np.ascontiguousarray(x), "w_in": w, "c_in": c16}

    nc = _bacc.Bacc("TRN2", target_bir_lowering=False, num_devices=1)
    args = [nc.dram_tensor(n, a.shape, _mybir.dt.from_np(a.dtype), kind="ExternalInput").ap() for n, a in arrays.items()]
    args.append(nc.dram_tensor("out_0", (P, NBLK * DM), _mybir.dt.float32, kind="ExternalOutput").ap())
    build(nc, *args)
    got = _run(nc, [arrays], core_ids=[0]).results[0]["out_0"]
    return got.reshape(P, NBLK, DM).transpose(1, 0, 2).reshape(BATCH, SEQ, DM)
```

```python
from contextlib import ExitStack

import numpy as np
import concourse.bass as bass
from concourse import mybir

F32, BF16, I32, U16 = mybir.dt.float32, mybir.dt.bfloat16, mybir.dt.int32, mybir.dt.uint16
ALU, ACT, AX = mybir.AluOpType, mybir.ActivationFunctionType, mybir.AxisListType

P = 128
BATCH, SEQ, DM = 8, 256, 128
NBLK = BATCH * SEQ // P
NTOK = BATCH * SEQ
BANK = 512
NGRP = NTOK // BANK
GB = BANK // P
NH, HD, NS = 4, 64, 64
HALF = NS // 2
NPAIR = NH * HD // P
NE, EF, SF = 16, 128, 512
NSC = SF // P
NSLOT = NBLK + NE - 1
EARLY = 3
DI, DS, DC, DR = 256, 16, 4, 8
NCH = DI // P
PADT = SEQ + DC - 1
HTOK = NTOK // 2
ROUND = 1.5 * 2.0 ** 23
MASKED = -1e30

_W_EARLY = [("in_a", 1028), ("dt_bias", NH), ("a_log_a", NH), ("ident", P), ("tri", 2 * P), ("shift", P),
            ("shift_in", P), ("inv_freq", HALF), ("norm_w", NPAIR), ("out_a", NPAIR * DM)]
_W_LATE = [("router", NE), ("shared_gate", SF), ("shared_up", SF), ("shared_down", NSC * DM),
           ("gate_up", NE * 2 * EF), ("down", NE * DM), ("rev_expert", NE), ("keep", NE * NBLK), ("slot", NSLOT),
           ("in_b", 2 * DI), ("conv_w", DC * DI), ("conv_b", NCH), ("x_b", NCH * (2 * DS + DR)), ("dt_w", DI),
           ("dt_b", NCH), ("a_log_b", NCH * DS), ("d_b", NCH), ("out_b", NCH * DM)]
_C16 = [("ident16", P), ("tri16", P), ("ones16", P), ("mask16", 3 * P), ("pick_head", NH * P),
        ("pick_row", 2 * DS * P)]


def offsets(table):
    at, found = 0, {}
    for name, width in table:
        found[name] = (at, width)
        at += width
    return found, at


W_AT, W_COLS = offsets(_W_EARLY + _W_LATE)
W_EARLY_COLS = offsets(_W_EARLY)[1]
C_AT, C_COLS = offsets(_C16)
C_EARLY_COLS = C_AT["pick_row"][0]


class Engine:

    def __init__(self, engine, semaphore):
        self.engine, self.semaphore, self.count, self.seen = engine, semaphore, 0, {}

    def after(self, *marks):
        for mark in marks:
            if isinstance(mark, list):
                self.after(*mark)
            elif mark is not None and self.seen.get(mark[0].name, 0) < mark[1]:
                self.engine.wait_ge(mark[0], mark[1])
                self.seen[mark[0].name] = mark[1]
        return self.engine

    def did(self, instruction):
        instruction.then_inc(self.semaphore, 1)
        self.count += 1
        return self.last()

    def last(self):
        return (self.semaphore, self.count)


class Transfers:

    def __init__(self, semaphore):
        self.semaphore, self.count = semaphore, 0

    def sent(self, dma):
        dma.then_inc(self.semaphore, 16)
        self.count += 16
        return (self.semaphore, self.count)

    def last(self):
        return (self.semaphore, self.count)


class Ring:

    def __init__(self, banks):
        self.banks, self.freed, self.turn = banks, [None] * len(banks), 0

    def take(self):
        self.turn += 1
        return self.banks[(self.turn - 1) % len(self.banks)], self.freed[(self.turn - 1) % len(self.banks)]

    def release(self, bank, mark):
        self.freed[self.banks.index(bank)] = mark


def build(nc, x_in, w_in, c_in, out):
    with ExitStack() as stack:
        def sb(name, shape, dtype=F32):
            return stack.enter_context(nc.sbuf_tensor(name, shape, dtype))

        def sem(name):
            return stack.enter_context(nc.semaphore(name))

        pe, dve = Engine(nc.tensor, sem("pe_done")), Engine(nc.vector, sem("dve_done"))
        act, pool = Engine(nc.scalar, sem("act_done")), Engine(nc.gpsimd, sem("pool_done"))
        sp = Engine(nc.sync, sem("sp_done"))

        psum = stack.enter_context(nc.psum_tensor("psum", [P, 8, BANK], F32))
        x = sb("x", [P, NBLK, DM])
        xn = sb("xn", [P, NBLK, DM])
        xnt = sb("xnt", [P, BATCH, PADT])
        w = sb("w", [P, W_COLS])
        c16 = sb("c16", [P, C_COLS], BF16)
        stats = sb("stats", [P, NBLK, 6])
        moments = sb("moments", [P, NBLK, 2])
        deviation = sb("deviation", [P, NBLK])
        rstd = sb("rstd", [P, NBLK])
        consts = sb("consts", [P, 4])
        zeros = sb("zeros", [P, DM])
        ARENA = 30000
        arena = sb("arena", [P, ARENA])
        sorted_x = [nc.dram_tensor(f"sorted_x{i}", [NSLOT * P, DM], F32, kind="Internal").ap() for i in range(2)]
        sorted_y = [nc.dram_tensor(f"sorted_y{i}", [NSLOT * P, DM], F32, kind="Internal").ap() for i in range(2)]

        def wt(name, rows=slice(0, P)):
            at, width = W_AT[name]
            return w[rows, at:at + width]

        def ct(name, rows=slice(0, P)):
            at, width = C_AT[name]
            return c16[rows, at:at + width]

        eps_ln, eps_rms, quarter_turn, one = (consts[:, i:i + 1] for i in range(4))
        ident, tri = wt("ident"), wt("tri")
        x_cols = x[:].rearrange("p b c -> p (b c)")
        xnt_tokens = xnt[:, :, DC - 1:PADT]

        def xnt_block(j):
            return xnt[:, j // 2, DC - 1 + P * (j % 2):DC - 1 + P * (j % 2) + P]

        def xnt_group(g):
            return xnt_tokens[:, 2 * g:2 * g + 2, :]

        measured = [None] * NGRP

        def measure(g, ready):
            blocks = range(GB * g, GB * g + GB)
            dve.after(ready)
            for j in blocks:
                stat = dve.did(nc.vector.bn_stats(stats[:, j, :], x[:, j, :]))
            dve.after(stat)
            for j in blocks:
                measured[g] = dve.did(nc.vector.bn_aggr(moments[:, j, :], stats[:, j, :]))

        load_x = [Transfers(sem(f"load_x{g}")) for g in range(NGRP)]
        load_early, load_late, zero_fill = Transfers(sem("load_early")), Transfers(sem("load_late")), Transfers(sem("zero_fill"))
        for g in range(NGRP):
            cols = slice(BANK * g, BANK * g + BANK)
            load_x[g].sent(nc.sync.dma_start(x_cols[:, cols], x_in[:, cols]))
        load_early.sent(nc.scalar.dma_start(w[:, 0:W_EARLY_COLS], w_in[:, 0:W_EARLY_COLS]))
        load_early.sent(nc.scalar.dma_start(c16[:, 0:C_EARLY_COLS].bitcast(U16), c_in[:, 0:C_EARLY_COLS]))
        sp.after(load_early.last())
        load_late.sent(nc.sync.dma_start(w[:, W_EARLY_COLS:W_COLS], w_in[:, W_EARLY_COLS:W_COLS]))
        load_late.sent(nc.sync.dma_start(c16[:, C_EARLY_COLS:C_COLS].bitcast(U16), c_in[:, C_EARLY_COLS:C_COLS]))
        zeroed = dve.did(nc.vector.memset(zeros[:], 0.0))
        for buffer in sorted_x:
            zero_fill.sent(sp.after(zeroed).dma_start(buffer.rearrange("(s p) c -> p s c", p=P),
                                        zeros[:].unsqueeze(1).to_broadcast([P, NSLOT, DM])))
        for value, tile in ((1e-5, eps_ln), (1e-6, eps_rms), (float(np.pi / 2), quarter_turn), (1.0, one)):
            consts_set = pool.did(nc.gpsimd.memset(tile, value))
        pads_set = pool.did(nc.gpsimd.memset(xnt[:, :, 0:DC - 1], 0.0))
        for g in range(NGRP):
            measure(g, load_x[g].last())
        for e in (pe, dve, act, pool):
            e.after(load_early.last(), consts_set, pads_set)

        def next_layer(*more):
            marks = [e.last() for e in (pe, dve, act, pool)] + list(more)
            for e in (pe, dve, act, pool):
                e.after(marks)

        def carve():
            taken = [0]

            def piece(columns, rows=slice(0, P)):
                taken[0] += columns
                assert taken[0] <= ARENA, taken
                return arena[rows, taken[0] - columns:taken[0]]
            return piece

        def normalise():
            root = act.did(act.after(measured).activation(deviation[:], moments[:, :, 1], ACT.Sqrt, bias=eps_ln))
            inverse = dve.did(dve.after(root).reciprocal(rstd[:], deviation[:]))
            dve.after(inverse)
            ring = Ring([psum[:, i, :] for i in range(2)])
            marks = []
            for g in range(NGRP):
                for j in range(GB * g, GB * g + GB):
                    scaled = dve.did(nc.vector.tensor_scalar(xn[:, j, :], x[:, j, :], moments[:, j, 0:1], rstd[:, j:j + 1],
                                                             ALU.subtract, ALU.mult))
                bank = psum[:, g % 2, :]
                pe.after(scaled, marks[g - 2] if g >= 2 else None)
                for j in range(GB):
                    turned = pe.did(nc.tensor.transpose(bank[:, P * j:P * j + P], xn[:, GB * g + j, :], ident))
                marks.append(act.did(act.after(turned).activation(
                    xnt_group(g), bank.rearrange("p (s t) -> p s t", s=2), ACT.Copy)))
            return marks

        def state_space():
            piece = carve()
            z_silu = piece(NPAIR * NTOK).rearrange("p (c t) -> p c t", c=NPAIR)
            xw = piece(NBLK * NH * HD).rearrange("p (j h c) -> p j h c", j=NBLK, h=NH)
            rotated = [[piece(NTOK) for _ in range(2)] for _ in range(2)]
            cosine, sine = piece(NTOK), piece(NTOK)
            gated = cosine_and_sine = None
            dt = piece(NBLK * NH)
            small = [piece(NBLK * NH) for _ in range(8)]
            cum = piece(NBLK * NH)
            neg_cum, neg_u = piece(NBLK * NH), piece(NBLK * NH)
            a_row = piece(NH)
            parts = piece(NBLK * 3 * NH // 2).bitcast(BF16).rearrange("p (j q h) -> p j q h", j=NBLK, q=3)
            cum_parts = piece(NTOK // 2, slice(0, 3 * NH)).bitcast(BF16)
            products = [piece(BANK) for _ in range(8)]
            decay = [piece(3 * P) for _ in range(4)]
            mixed = [piece(3 * P) for _ in range(3)]
            out_w = piece(NPAIR * DM)
            freq_dt = xw.rearrange("p j h c -> p (j h c)")[:, 0:NTOK]
            turns = xw.rearrange("p j h c -> p (j h c)")[:, NTOK:2 * NTOK]
            n4 = NBLK * NH

            normed = normalise()
            in_a = wt("in_a")
            z_w, bc_w = in_a[:, 0:2 * P], in_a[:, 2 * P:6 * P]
            xr_w, dt_w = in_a[:, 6 * P:8 * P], in_a[:, 8 * P:8 * P + NH]

            dt_bank, aux_bank = psum[:, 2, 0:n4], psum[:, 3, :]
            pe.after(normed)
            for j in range(NBLK):
                raw_ready = pe.did(nc.tensor.matmul(dt_bank[:, NH * j:NH * j + NH], xnt_block(j), dt_w, start=True, stop=True))
            v, least, e, log1p, shifted, total, inverse, half = small

            def heads(t):
                return t.rearrange("p (j h) -> p j h", h=NH)

            def per_head(row):
                return row.unsqueeze(1).to_broadcast([P, NBLK, NH])

            m = dve.did(dve.after(raw_ready).tensor_tensor(heads(v), heads(dt_bank), per_head(wt("dt_bias")), ALU.add))
            m = dve.did(dve.after(m).scalar_tensor_tensor(least, v, -1.0, v, ALU.mult, ALU.min))
            e_ready = act.did(act.after(m).activation(e, least, ACT.Exp))
            a_exp = act.did(nc.scalar.activation(a_row, wt("a_log_a"), ACT.Exp))
            log_ready = act.did(act.after(e_ready).activation(log1p, e, ACT.Ln, bias=one))
            dt_ready = dve.did(dve.after(log_ready).scalar_tensor_tensor(dt, v, 0.0, log1p, ALU.max, ALU.add))
            neg_dta = half
            m = dve.did(dve.after(a_exp, dt_ready).tensor_tensor(heads(neg_dta), heads(dt), per_head(a_row), ALU.mult))
            pe.after(m)
            nxt, run = aux_bank[:, 0:n4], aux_bank[:, n4:2 * n4]
            odd_dt, even_cols = heads(dt)[:, 1::2, :], heads(nxt)[:, 0::2, :]
            nc.tensor.matmul(nxt, wt("shift"), dt, start=True, stop=True)
            nc.tensor.matmul(even_cols, wt("shift_in"), odd_dt, start=False, stop=True, skip_group_check=True)
            nc.tensor.matmul(run, tri[:, 0:P], neg_dta, start=False, stop=True, skip_group_check=True)
            sums = pe.did(nc.tensor.matmul(heads(run)[:, 1::2, :], tri[:, P:2 * P], heads(neg_dta)[:, 0::2, :],
                                           start=False, stop=True, skip_group_check=True))
            dve.after(sums)
            m_shift = dve.did(nc.vector.tensor_copy(shifted, nxt))
            m_neg = dve.did(nc.vector.tensor_copy(neg_cum, run))
            m_cum = dve.did(nc.vector.tensor_scalar(cum, run, -1.0, None, ALU.mult))
            m_tot = dve.did(dve.after(m_shift).tensor_tensor(total, dt, shifted, ALU.add))
            m = dve.did(dve.after(m_tot).tensor_scalar(e, total, 1e-30, None, ALU.max))
            m = dve.did(dve.after(m).reciprocal(inverse, e))
            m_u = dve.did(dve.after(m).scalar_tensor_tensor(neg_u, shifted, -1.0, inverse, ALU.mult, ALU.mult))
            weight_ready = dve.did(nc.vector.tensor_scalar(v, total, 0.5, None, ALU.mult))
            parts_of = parts
            m1 = dve.did(dve.after(m_cum).tensor_copy(parts_of[:, :, 0, :], heads(cum)))
            m2 = dve.did(dve.after(m1).tensor_tensor(heads(log1p), heads(cum), parts_of[:, :, 0, :], ALU.subtract))
            m3 = dve.did(dve.after(m2).tensor_copy(parts_of[:, :, 1, :], heads(log1p)))
            m4 = dve.did(dve.after(m3).tensor_tensor(parts_of[:, :, 2, :], heads(log1p), parts_of[:, :, 1, :], ALU.subtract))
            pe.after(m4)
            for k in range(2):
                for j in range(8):
                    t = psum[:, 4 + k, :].bitcast(BF16)[0:3 * NH, P * j:P * j + P]
                    turned = pe.did(nc.tensor.transpose(t, parts_of[:, 8 * k + j, :, :].rearrange("p q h -> p (q h)"), ct("ident16")))
                parts_ready = act.did(act.after(turned).activation(
                    cum_parts[:, 8 * P * k:8 * P * k + 8 * P], psum[:, 4 + k, :].bitcast(BF16)[0:3 * NH, :], ACT.Copy))

            m = pool.did(pool.after(dt_ready).tensor_tensor(
                freq_dt.rearrange("p (j f) -> p j f", f=HALF), dt.unsqueeze(2).to_broadcast([P, n4, HALF]),
                wt("inv_freq").unsqueeze(1).to_broadcast([P, n4, HALF]), ALU.mult))
            pe.after(m)
            cos_cols, sin_cols = products[0], None
            angle_ring = Ring([psum[:, i, :] for i in (6, 7)])
            turned_marks = []
            rounds = [products[i] for i in range(4)]
            reduced_free = [None, None]
            for g in range(NGRP):
                bank, free = angle_ring.take()
                pe.after(free)
                for s in range(2):
                    j = GB * g + 2 * s
                    cols = bank[:, SEQ * s:SEQ * s + SEQ]
                    nc.tensor.matmul(cols, freq_dt[:, P * j:P * j + P], tri, start=(s == 0), stop=True, skip_group_check=True)
                    angles = pe.did(nc.tensor.matmul(cols[:, P:SEQ], freq_dt[:, P * j + P:P * j + 2 * P], tri[:, 0:P],
                                                     start=False, stop=True, skip_group_check=True))
                a, b = rounds[0], rounds[1]
                ns, ncos = sine[:, BANK * g:BANK * g + BANK], cosine[:, BANK * g:BANK * g + BANK]
                dve.after(angles)
                m1 = dve.did(nc.vector.tensor_scalar(a, bank, ROUND, None, ALU.add))
                m2 = dve.did(nc.vector.tensor_scalar(b, bank, 0.25, ROUND, ALU.add, ALU.add))
                m1 = dve.did(dve.after(m1).scalar_tensor_tensor(ns, a, ROUND, bank, ALU.subtract, ALU.subtract))
                m2 = dve.did(dve.after(m2).scalar_tensor_tensor(ncos, b, ROUND, bank, ALU.subtract, ALU.subtract))
                dve.after(m2)
                angle_ring.release(bank, m2)
                turned_marks.append(m2)
            act.after(turned_marks[-1])
            full_turn = 6.283185
            trig = []
            for g in range(NGRP):
                cols = slice(BANK * g, BANK * g + BANK)
                nc.scalar.activation(sine[:, cols], sine[:, cols], ACT.Sin, scale=-full_turn)
                trig.append(act.did(nc.scalar.activation(cosine[:, cols], cosine[:, cols], ACT.Sin, scale=-full_turn,
                                                         bias=quarter_turn)))

            ring = Ring([psum[:, i, :] for i in range(8)])
            pe.after(parts_ready, turned_marks[-1])
            for g in range(NGRP):
                for c in range(NPAIR):
                    bank, free = ring.take()
                    z_ready = pe.did(pe.after(free).matmul(bank, z_w[:, P * c:P * c + P], xnt_group(g), start=True, stop=True))
                    ring.release(bank, act.did(act.after(z_ready).activation(z_silu[:, c, BANK * g:BANK * g + BANK], bank, ACT.Silu)))
            product_free = [m2] * 8
            rotated_ready = []
            for g in range(NGRP):
                cols = slice(BANK * g, BANK * g + BANK)
                for k in range(2):
                    p0, p1, p2, p3 = products[4 * k:4 * k + 4]
                    bank0, free0 = ring.take()
                    bank1, free1 = ring.take()
                    r0 = pe.did(pe.after(free0).matmul(bank0, bc_w[:, 2 * P * k:2 * P * k + P], xnt_group(g), start=True, stop=True))
                    r1 = pe.did(pe.after(free1).matmul(bank1, bc_w[:, 2 * P * k + P:2 * P * k + 2 * P], xnt_group(g),
                                                       start=True, stop=True))
                    dve.after(r0, trig[g], product_free[k])
                    nc.vector.tensor_tensor(p0, bank0, cosine[:, cols], ALU.mult)
                    m = dve.did(nc.vector.tensor_tensor(p2, bank0, sine[:, cols], ALU.mult))
                    ring.release(bank0, m)
                    dve.after(r1)
                    m0 = dve.did(nc.vector.tensor_tensor(p1, bank1, sine[:, cols], ALU.mult))
                    m1 = dve.did(nc.vector.tensor_tensor(p3, bank1, cosine[:, cols], ALU.mult))
                    ring.release(bank1, m1)
                    pool.after(m1)
                    nc.gpsimd.tensor_tensor(rotated[k][0][:, cols], p0, p1, ALU.subtract)
                    product_free[k] = pool.did(nc.gpsimd.tensor_tensor(rotated[k][1][:, cols], p2, p3, ALU.add))
                    rotated_ready.append(product_free[k])
            for j in range(0, NBLK, 2):
                bank, free = ring.take()
                pe.after(free)
                for i in range(2):
                    r = pe.did(nc.tensor.matmul(bank[:, 2 * P * i:2 * P * i + 2 * P], xnt_block(j + i), xr_w, start=True, stop=True))
                dve.after(r, turned_marks[-1], weight_ready)
                xw_ready = dve.did(nc.vector.tensor_tensor(
                    xw[:, j:j + 2, :, :].rearrange("p j h c -> p (j h) c"), bank.rearrange("p (q c) -> p q c", c=HD),
                    v[:, NH * j:NH * j + 2 * NH].unsqueeze(2).to_broadcast([P, 2 * NH, HD]), ALU.mult))
                ring.release(bank, xw_ready)

            next_layer()
            exponents = Ring([psum[:, i, :] for i in range(3)])
            scores = Ring([psum[:, i, :] for i in range(3, 6)])
            outputs = Ring([psum[:, i, :] for i in range(6, 8)])
            units = [(b, h) for b in range(BATCH) for h in range(NH)]
            decay_ready, decay_free = [None] * len(units), [None] * len(decay)
            mixed_ready, mixed_free = [None] * len(units), [None] * len(mixed)

            def decays(i):
                b, h = units[i]
                bank, free = exponents.take()
                pe.after(free)
                pick = ct("pick_head", slice(0, 3 * NH))[:, P * h:P * h + P]
                t0, tm, t1 = SEQ * b, SEQ * b + P, SEQ * b + SEQ
                nc.tensor.matmul(bank[:, 0:2 * P], pick, cum_parts[:, t0:t1], start=True, stop=True, skip_group_check=True)
                nc.tensor.matmul(bank[:, 2 * P:3 * P], pick, cum_parts[:, tm:t1], start=False, stop=True, skip_group_check=True)
                exponent = pe.did(nc.tensor.matmul(bank[:, 0:3 * P], ct("ident16"), ct("mask16"), start=False, stop=True,
                                                   skip_group_check=True))
                k = i % len(decay)
                d, j = decay[k], 2 * b
                act.after(exponent, decay_free[k])
                nc.scalar.activation(d[:, 0:2 * P], bank[:, 0:2 * P], ACT.Exp, bias=neg_cum[:, NH * j + h:NH * j + h + 1])
                decayed = act.did(nc.scalar.activation(d[:, 2 * P:3 * P], bank[:, 2 * P:3 * P], ACT.Exp,
                                                       bias=neg_cum[:, NH * (j + 1) + h:NH * (j + 1) + h + 1]))
                exponents.release(bank, decayed)
                dve.after(decayed)
                for q, cols in ((0, slice(0, P)), (1, slice(2 * P, 3 * P))):
                    decay_ready[i] = dve.did(nc.vector.scalar_tensor_tensor(
                        d[:, cols], ident, neg_u[:, NH * (j + q) + h:NH * (j + q) + h + 1], d[:, cols], ALU.mult, ALU.add))

            def score(i):
                b, h = units[i]
                rows = slice(HALF * h, HALF * h + HALF)
                t0, tm, t1 = SEQ * b, SEQ * b + P, SEQ * b + SEQ
                bank, free = scores.take()
                pe.after(free)
                for k in range(2):
                    b_rows, c_rows = rotated[0][k][rows, :], rotated[1][k][rows, :]
                    nc.tensor.matmul(bank[:, 0:2 * P], b_rows[:, t0:tm], c_rows[:, t0:t1], start=(k == 0), stop=(k == 1),
                                     skip_group_check=True)
                for k in range(2):
                    b_rows, c_rows = rotated[0][k][rows, :], rotated[1][k][rows, :]
                    scored = nc.tensor.matmul(bank[:, 2 * P:3 * P], b_rows[:, tm:t1], c_rows[:, tm:t1], start=False,
                                              stop=(k == 1), skip_group_check=True)
                scored = pe.did(scored)
                k = i % len(mixed)
                dve.after(scored, decay_ready[i], mixed_free[k])
                mixed_ready[i] = dve.did(nc.vector.tensor_tensor(mixed[k], bank[:, 0:3 * P], decay[i % len(decay)], ALU.mult))
                scores.release(bank, mixed_ready[i])
                decay_free[i % len(decay)] = mixed_ready[i]

            y_bank = [None, None]

            def output(i):
                b, h = units[i]
                if h == 0:
                    y_bank[0], y_bank[1] = outputs.take()
                bank = y_bank[0]
                pe.after(mixed_ready[i], y_bank[1])
                rows, at = slice(HD * (h % 2), HD * (h % 2) + HD), SEQ * (h // 2)
                g = mixed[i % len(mixed)]
                nc.tensor.matmul(bank[rows, at:at + SEQ], xw[:, 2 * b, h, :], g[:, 0:2 * P], start=True, stop=True,
                                 skip_group_check=True)
                m = pe.did(nc.tensor.matmul(bank[rows, at + P:at + SEQ], xw[:, 2 * b + 1, h, :], g[:, 2 * P:3 * P],
                                            start=False, stop=True, skip_group_check=True))
                mixed_free[i % len(mixed)] = m
                if h == NH - 1:
                    gate = z_silu[:, :, SEQ * b:SEQ * b + SEQ]
                    gated = dve.did(dve.after(m).tensor_tensor(gate, bank.rearrange("p (c t) -> p c t", c=NPAIR), gate, ALU.mult))
                    outputs.release(bank, gated)

            ahead = 2
            for i in range(-ahead, len(units) + 1):
                if i + ahead < len(units):
                    decays(i + ahead)
                if 0 <= i < len(units):
                    score(i)
                if i >= 1:
                    output(i - 1)

            for c in range(NPAIR):
                w_ready = dve.did(nc.vector.tensor_scalar(out_w[:, DM * c:DM * c + DM], wt("out_a")[:, DM * c:DM * c + DM],
                                                          wt("norm_w")[:, c:c + 1], None, ALU.mult))
            next_layer()
            squares = xw.rearrange("p j h c -> p (j h c)").rearrange("p (c t) -> p c t", c=NPAIR)
            sum_bank = psum[:, 0, 0:NBLK]
            for b in range(BATCH):
                cols = slice(SEQ * b, SEQ * b + SEQ)
                m = act.did(nc.scalar.activation(squares[:, :, cols], z_silu[:, :, cols], ACT.Square))
                pe.after(m)
                for j in (2 * b, 2 * b + 1):
                    for c in range(NPAIR):
                        s = nc.tensor.matmul(sum_bank[:, j:j + 1], squares[:, c, P * j:P * j + P], tri[:, P:P + 1],
                                             start=(c == 0), stop=(c == NPAIR - 1))
            summed = pe.did(s)
            root = act.did(act.after(summed).activation(deviation[:], sum_bank, ACT.Sqrt, bias=eps_rms, scale=1.0 / (NH * HD)))
            scale_ready = dve.did(dve.after(root).reciprocal(rstd[:], deviation[:]))
            ring = Ring([psum[:, i, :] for i in range(1, 8)])
            dve.after(scale_ready)
            for g in range(NGRP):
                bank, free = ring.take()
                pe.after(free)
                for q in range(GB):
                    j = GB * g + q
                    for c in range(NPAIR):
                        r = nc.tensor.matmul(bank[:, P * q:P * q + P], z_silu[:, c, P * j:P * j + P],
                                             out_w[:, DM * c:DM * c + DM], start=(c == 0), stop=(c == NPAIR - 1))
                r = pe.did(r)
                dve.after(r)
                for q in range(GB):
                    j = GB * g + q
                    added = dve.did(nc.vector.scalar_tensor_tensor(x[:, j, :], bank[:, P * q:P * q + P], rstd[:, j:j + 1],
                                                                   x[:, j, :], ALU.mult, ALU.add))
                ring.release(bank, added)
                measure(g, added)

        def experts(turn):
            piece = carve()
            xs_rows = piece(NSLOT * DM).rearrange("p (s c) -> p s c", s=NSLOT)
            xs_t = piece(NSLOT * P)
            y_rows = piece(NSLOT * DM).rearrange("p (s c) -> p s c", s=NSLOT)
            scaled = piece(NBLK * DM).rearrange("p (j c) -> p j c", j=NBLK)
            gathered = piece(NBLK * DM).rearrange("p (j c) -> p j c", j=NBLK)
            shared_act = [piece(NSC * BANK).rearrange("p (c t) -> p c t", c=NSC) for _ in range(2)]
            shared_gate = [piece(BANK) for _ in range(2)]
            gate = [piece(2 * EF) for _ in range(2)]
            hidden = [piece(2 * EF) for _ in range(2)]
            hidden_t = [piece(2 * EF) for _ in range(2)]
            logit_max, best, score, position = (piece(NBLK) for _ in range(4))
            position_int = piece(NBLK).bitcast(I32)
            chosen, one_hot, totals, running, base, rank = (piece(NBLK * NE) for _ in range(6))
            one_hot16 = piece(NBLK * NE // 2).bitcast(BF16)
            n_slots, end_slot, start_row = (piece(NE) for _ in range(3))
            passed = piece(NSLOT * NE)
            expert = piece(NSLOT)
            expert_int = piece(NSLOT).bitcast(I32)

            normed = normalise()

            def by_token(t):
                return t.rearrange("p (j n) -> p j n", n=NE)

            def by_expert(t):
                return t.rearrange("p (n j) -> p j n", j=NBLK)

            logits = psum[:, 2, 0:NBLK * NE]
            pe.after(normed)
            for j in range(NBLK):
                r = nc.tensor.matmul(logits[:, NE * j:NE * j + NE], xnt_block(j), wt("router"), start=True, stop=True)
            r = pe.did(r)
            m_max = dve.did(dve.after(r).tensor_reduce(logit_max, by_token(logits), AX.X, ALU.max))
            m = dve.did(dve.after(m_max).tensor_tensor(
                by_token(chosen), by_token(logits), logit_max.unsqueeze(2).to_broadcast([P, NBLK, NE]), ALU.is_equal))
            rev = wt("rev_expert").unsqueeze(1).to_broadcast([P, NBLK, NE])
            m = dve.did(dve.after(m).tensor_tensor(by_token(rank), by_token(chosen), rev, ALU.mult))
            m = dve.did(dve.after(m).tensor_reduce(best, by_token(rank), AX.X, ALU.max))
            m_hot = dve.did(dve.after(m).tensor_tensor(
                by_token(one_hot), rev, best.unsqueeze(2).to_broadcast([P, NBLK, NE]), ALU.is_equal))
            m_hot16 = dve.did(dve.after(m_hot).tensor_copy(one_hot16, one_hot))
            scored = act.did(act.after(m_max).activation(score, logit_max, ACT.Sigmoid))
            pe.after(m_hot16)
            in_block, block_total = psum[:, 3, 0:NBLK * NE], psum[:, 4, 0:NBLK * NE]
            nc.tensor.matmul(in_block, ct("tri16"), one_hot16, start=True, stop=True)
            r = pe.did(nc.tensor.matmul(block_total, ct("ones16"), one_hot16, start=True, stop=True))
            scaled_ready = dve.did(dve.after(scored).tensor_tensor(
                scaled, xn[:], score.unsqueeze(2).to_broadcast([P, NBLK, DM]), ALU.mult))
            m = dve.did(dve.after(r).tensor_copy(by_expert(totals), by_token(block_total)))
            m_run = dve.did(dve.after(m).tensor_tensor_scan(running, wt("keep"), totals, 0.0, ALU.mult, ALU.add))
            counts = running.rearrange("p (n j) -> p n j", j=NBLK)[:, :, NBLK - 1]
            m = dve.did(dve.after(m_run).tensor_scalar(n_slots, counts, 1.0 / P, (P - 1.0) / P - (P - 1.0) / (2 * P), ALU.mult, ALU.add))
            m = dve.did(dve.after(m).tensor_scalar(n_slots, n_slots, ROUND, -ROUND, ALU.add, ALU.add))
            m_end = dve.did(dve.after(m).tensor_tensor_scan(end_slot, tri[:, P:P + NE], n_slots, 0.0, ALU.mult, ALU.add))
            m = dve.did(dve.after(m_end).tensor_tensor(start_row, end_slot, n_slots, ALU.subtract))
            m = dve.did(dve.after(m).tensor_scalar(start_row, start_row, float(P), -1.0, ALU.mult, ALU.add))
            m = dve.did(dve.after(m).tensor_tensor(base, running, totals, ALU.subtract))
            m = dve.did(dve.after(m).tensor_tensor(base.rearrange("p (n j) -> p n j", j=NBLK), base.rearrange("p (n j) -> p n j", j=NBLK),
                                                   start_row.unsqueeze(2).to_broadcast([P, NE, NBLK]), ALU.add))
            m = dve.did(dve.after(m).tensor_tensor(by_token(rank), by_token(in_block), by_expert(base), ALU.add))
            m = dve.did(dve.after(m).tensor_tensor(rank, rank, one_hot, ALU.mult))
            m = dve.did(dve.after(m).tensor_reduce(position, by_token(rank), AX.X, ALU.add))
            placed = dve.did(dve.after(m).tensor_copy(position_int, position))
            m = dve.did(dve.after(m_end).tensor_tensor(
                passed.rearrange("p (s n) -> p s n", n=NE), wt("slot").unsqueeze(2).to_broadcast([P, NSLOT, NE]),
                end_slot.unsqueeze(1).to_broadcast([P, NSLOT, NE]), ALU.is_ge))
            m = dve.did(dve.after(m).tensor_reduce(expert, passed.rearrange("p (s n) -> p s n", n=NE), AX.X, ALU.add))
            m = dve.did(dve.after(m).tensor_scalar(expert, expert, float(NE - 1), None, ALU.min))
            expert_ready = dve.did(dve.after(m).tensor_copy(expert_int, expert))

            scatter, fetch = Transfers(sem(f"scatter{turn}")), Transfers(sem(f"fetch{turn}"))
            store, gather = Transfers(sem(f"store{turn}")), [Transfers(sem(f"gather{turn}_{g}")) for g in range(NGRP)]
            pool.after(placed, scaled_ready, zero_fill.last())
            for j in range(NBLK):
                scatter.sent(nc.gpsimd.indirect_dma_start(
                    sorted_x[turn], bass.IndirectOffsetOnAxis(position_int[:, j:j + 1], 0), scaled[:, j, :], None))
            fetch.sent(sp.after(scatter.last()).dma_start(xs_rows, sorted_x[turn].rearrange("(s p) c -> p s c", p=P)))

            up_ring = Ring([psum[:, i, :] for i in (5, 6)])
            gate_ring = Ring([psum[:, i, :] for i in (7, 0)])
            down_ring = Ring([psum[:, i, :] for i in (1, 2)])
            pe.after(placed)
            shared_added = [None] * NGRP
            down_done = [None] * NGRP
            gate_free = [None, None]

            def shared_down(g):
                bank, free = down_ring.take()
                pe.after(free, hidden_ready[g])
                for q in range(GB):
                    for c in range(NSC):
                        r = nc.tensor.matmul(bank[:, P * q:P * q + P], shared_act[g % 2][:, c, P * q:P * q + P],
                                             wt("shared_down")[:, DM * c:DM * c + DM], start=(c == 0), stop=(c == NSC - 1))
                down_done[g] = pe.did(r)
                cols = x_cols[:, BANK * g:BANK * g + BANK]
                shared_added[g] = dve.did(dve.after(down_done[g]).tensor_tensor(cols, bank, cols, ALU.add))
                down_ring.release(bank, shared_added[g])

            hidden_ready = [None] * NGRP
            def shared_up_gate(g):
                for c in range(NSC):
                    cols = slice(P * c, P * c + P)
                    bank_g, free = gate_ring.take()
                    r = pe.did(pe.after(free).matmul(bank_g, wt("shared_gate")[:, cols], xnt_group(g), start=True, stop=True))
                    sg = shared_gate[c % 2]
                    m = act.did(act.after(r, gate_free[c % 2]).activation(sg, bank_g, ACT.Silu))
                    gate_ring.release(bank_g, m)
                    bank_u, free = up_ring.take()
                    r = pe.did(pe.after(free).matmul(bank_u, wt("shared_up")[:, cols], xnt_group(g), start=True, stop=True))
                    dve.after(r, m, down_done[g - 2] if g >= 2 else None)
                    hidden_ready[g] = dve.did(nc.vector.tensor_tensor(shared_act[g % 2][:, c, :], bank_u, sg, ALU.mult))
                    gate_free[c % 2] = hidden_ready[g]
                    up_ring.release(bank_u, hidden_ready[g])

            for g in range(EARLY):
                shared_up_gate(g)
                if g >= 1:
                    shared_down(g - 1)
            shared_down(EARLY - 1)

            next_layer(fetch.last())
            turn_ring = Ring([psum[:, i, :] for i in (0, 1)])
            turned_in = [None] * NSLOT
            for s0 in range(0, NSLOT, GB):
                n = min(GB, NSLOT - s0)
                bank, free = turn_ring.take()
                pe.after(free)
                for q in range(n):
                    r = nc.tensor.transpose(bank[:, P * q:P * q + P], xs_rows[:, s0 + q, :], ident)
                r = pe.did(r)
                m = act.did(act.after(r).activation(xs_t[:, P * s0:P * s0 + P * n], bank[:, 0:P * n], ACT.Copy))
                turn_ring.release(bank, m)
                for q in range(n):
                    turned_in[s0 + q] = m
            up_ring = Ring([psum[:, i, :] for i in (2, 3)])
            flip_ring = Ring([psum[:, i, :] for i in (4, 5)])
            down_ring = Ring([psum[:, i, :] for i in (6, 7)])
            pairs = [tuple(range(s, min(s + 2, NSLOT))) for s in range(0, NSLOT, 2)]
            chosen_expert = {}
            gate_up, down = wt("gate_up"), wt("down")
            hidden_free, flipped_free, gate_used = [None] * 2, [None] * 2, [None] * 2
            stage1, stage2 = {}, {}

            def expand(k):
                bank, free = up_ring.take()
                pe.after(free, [turned_in[s] for s in pairs[k]], expert_ready)
                for q, s in enumerate(pairs[k]):
                    chosen_expert[s] = nc.tensor.value_load(expert_int[0:1, s:s + 1], min_val=0, max_val=NE - 1)
                    r = nc.tensor.matmul(bank[:, 2 * EF * q:2 * EF * q + 2 * EF], xs_t[:, P * s:P * s + P],
                                         gate_up[:, bass.ds(chosen_expert[s] * (2 * EF), 2 * EF)], start=True, stop=True)
                r = pe.did(r)
                n = len(pairs[k])
                halves = bank.rearrange("p (q u f) -> p q u f", q=2, u=2)
                gt = gate[k % 2].rearrange("p (q f) -> p q f", q=2)[:, 0:n, :]
                m = act.did(act.after(r, gate_used[k % 2]).activation(gt, halves[:, 0:n, 0, :], ACT.Silu))
                hd = hidden[k % 2].rearrange("p (q f) -> p q f", q=2)[:, 0:n, :]
                m = dve.did(dve.after(m, hidden_free[k % 2]).tensor_tensor(hd, halves[:, 0:n, 1, :], gt, ALU.mult))
                gate_used[k % 2] = m
                up_ring.release(bank, m)
                stage1[k] = m

            def flip(k):
                bank, free = flip_ring.take()
                pe.after(free, stage1[k])
                n = len(pairs[k])
                for q in range(n):
                    r = nc.tensor.transpose(bank[:, P * q:P * q + P], hidden[k % 2][:, EF * q:EF * q + EF], ident)
                r = pe.did(r)
                hidden_free[k % 2] = r
                m = dve.did(dve.after(r, flipped_free[k % 2]).tensor_copy(hidden_t[k % 2][:, 0:P * n], bank[:, 0:P * n]))
                flip_ring.release(bank, m)
                stage2[k] = m

            stored = []

            def contract(k):
                bank, free = down_ring.take()
                pe.after(free, stage2[k])
                for q, s in enumerate(pairs[k]):
                    r = nc.tensor.matmul(bank[:, P * q:P * q + P], hidden_t[k % 2][:, P * q:P * q + P],
                                         down[:, bass.ds(chosen_expert[s] * DM, DM)], start=True, stop=True)
                r = pe.did(r)
                flipped_free[k % 2] = r
                n = len(pairs[k])
                s0 = pairs[k][0]
                m = act.did(act.after(r).activation(y_rows[:, s0:s0 + n, :], bank[:, 0:P * n].rearrange("p (q c) -> p q c", q=n), ACT.Copy))
                down_ring.release(bank, m)
                rows = sorted_y[turn].rearrange("(s p) c -> p s c", p=P)
                if k % 4 == 3 or k == len(pairs) - 1:
                    first = pairs[k - k % 4][0]
                    store.sent(sp.after(m).dma_start(rows[:, first:s0 + n, :], y_rows[:, first:s0 + n, :]))

            for k in range(len(pairs) + 2):
                if k < len(pairs):
                    expand(k)
                if 1 <= k <= len(pairs):
                    flip(k - 1)
                if k >= 2:
                    contract(k - 2)
            pool.after(store.last())
            for j in range(NBLK):
                gather[j // GB].sent(nc.gpsimd.indirect_dma_start(
                    gathered[:, j, :], None, sorted_y[turn], bass.IndirectOffsetOnAxis(position_int[:, j:j + 1], 0)))
            next_layer()
            up_ring, gate_ring, down_ring = (Ring([psum[:, i, :] for i in k]) for k in ((0, 1, 2), (3, 4, 5), (6, 7)))
            for g in range(EARLY, NGRP):
                shared_up_gate(g)
                shared_down(g)
            marks = []
            for g in range(NGRP):
                cols = slice(GB * g, GB * g + GB)
                marks.append(dve.did(dve.after(gather[g].last(), shared_added[g]).tensor_tensor(
                    x[:, cols, :], x[:, cols, :], gathered[:, cols, :], ALU.add)))
                if turn == 0:
                    measure(g, marks[g])
            return marks

        def selective_scan():
            piece = carve()
            u, z, dt, dtu = (piece(NCH * NTOK).rearrange("p (c t) -> p c t", c=NCH) for _ in range(4))
            u_w = piece(DC * DI)
            a_neg = piece(NCH * DS)
            nr = 2 * DS + DR
            low = piece(NTOK, slice(0, nr))
            rest = [piece(BANK, slice(0, 2 * DS)) for _ in range(2)]
            high16, mid16 = ([piece(BANK // 2, slice(0, 2 * DS)).bitcast(BF16) for _ in range(2)] for _ in range(2))
            rows16 = piece(NTOK // 2, slice(0, 6 * DS)).bitcast(BF16)
            spare = xn[:].rearrange("p j c -> p (j c)")
            decay = [[spare[:, BANK * (2 * c + i):BANK * (2 * c + i) + BANK] for i in range(2)] for c in range(NCH)]
            state = [[piece(BANK) for _ in range(3)] for _ in range(NCH)]
            c_row = [piece(BANK) for _ in range(3)]

            conv_w, in_b = wt("conv_w"), wt("in_b")
            for k in range(DC):
                w_ready = dve.did(nc.vector.tensor_tensor(u_w[:, DI * k:DI * k + DI], in_b[:, 0:DI], conv_w[:, DI * k:DI * k + DI],
                                                          ALU.mult))
            a_exp = act.did(nc.scalar.activation(a_neg, wt("a_log_b"), ACT.Exp))
            a_ready = dve.did(dve.after(a_exp).tensor_scalar(a_neg, a_neg, -1.0, None, ALU.mult))
            normed = normalise()
            pe.after(w_ready)
            ring = Ring([psum[:, i, :] for i in range(2, 8)])
            u_ready, low_ready = [[None] * NCH for _ in range(NGRP)], [None] * NGRP
            rest_free = [None] * 2

            def rows_of(g):
                cols = slice(BANK * g, BANK * g + BANK)
                bank, free = ring.take()
                pe.after(free, u_ready[g])
                for c in range(NCH):
                    r = nc.tensor.matmul(bank[0:nr, :], wt("x_b")[:, nr * c:nr * c + nr], u[:, c, cols], start=(c == 0), stop=(c == NCH - 1))
                r = pe.did(r)
                low_ready[g] = act.did(act.after(r).activation(low[:, cols], bank[0:nr, :], ACT.Copy))
                ring.release(bank, low_ready[g])
                lo, hi, mid, re = low[0:2 * DS, cols], high16[g % 2], mid16[g % 2], rest[g % 2]
                m = dve.did(dve.after(low_ready[g]).tensor_copy(hi, lo))
                m = dve.did(dve.after(m).tensor_tensor(re, lo, hi, ALU.subtract))
                m = dve.did(dve.after(m).tensor_copy(mid, re))
                dve.after(m)
                nc.vector.tensor_copy(rows16[0:2 * DS, cols], hi)
                nc.vector.tensor_copy(rows16[2 * DS:4 * DS, cols], mid)
                dve.did(nc.vector.tensor_tensor(rows16[4 * DS:6 * DS, cols], re, mid, ALU.subtract))

            for g in range(NGRP):
                cols = slice(BANK * g, BANK * g + BANK)
                pe.after(normed[g])
                for c in range(NCH):
                    bank, free = ring.take()
                    pe.after(free)
                    for k in range(DC):
                        r = nc.tensor.matmul(bank, u_w[:, DI * k + P * c:DI * k + P * c + P], xnt[:, 2 * g:2 * g + 2, k:k + SEQ],
                                             start=(k == 0), stop=(k == DC - 1))
                    r = pe.did(r)
                    u_ready[g][c] = act.did(act.after(r).activation(u[:, c, cols], bank, ACT.Silu, bias=wt("conv_b")[:, c:c + 1]))
                    ring.release(bank, u_ready[g][c])
                    bank, free = ring.take()
                    r = pe.did(pe.after(free).matmul(bank, in_b[:, DI + P * c:DI + P * c + P], xnt_group(g), start=True, stop=True))
                    m = act.did(act.after(r).activation(z[:, c, cols], bank, ACT.Silu))
                    ring.release(bank, m)
                if g >= 1:
                    rows_of(g - 1)
            rows_of(NGRP - 1)
            for g in range(NGRP):
                cols = slice(BANK * g, BANK * g + BANK)
                for c in range(NCH):
                    bank, free = ring.take()
                    r = pe.did(pe.after(free, low_ready[g]).matmul(
                        bank, wt("dt_w", slice(2 * DS, nr))[:, P * c:P * c + P], low[2 * DS:nr, cols], start=True, stop=True))
                    act.after(r)
                    nc.scalar.activation(dt[:, c, cols], bank, ACT.Abs, bias=wt("dt_b")[:, c:c + 1])
                    m = act.did(nc.scalar.activation(dtu[:, c, cols], bank, ACT.Relu, bias=wt("dt_b")[:, c:c + 1]))
                    ring.release(bank, m)
            act.after(m)
            for c in range(NCH):
                m = act.did(nc.scalar.activation(dt[:, c, :], dt[:, c, :], ACT.Exp, scale=-1.0))
            act.after(m)
            for g in range(NGRP):
                cols = slice(BANK * g, BANK * g + BANK)
                m = act.did(nc.scalar.activation(dt[:, :, cols], dt[:, :, cols], ACT.Ln, bias=one))
                m = dve.did(dve.after(m).tensor_tensor(dt[:, :, cols], dt[:, :, cols], dtu[:, :, cols], ALU.add))
                dve.did(dve.after(m, u_ready[g]).tensor_tensor(dtu[:, :, cols], dt[:, :, cols], u[:, :, cols], ALU.mult))

            for c in range(NCH):
                for i in range(2):
                    starts = decay[c][i].rearrange("p (s t) -> p s t", t=SEQ)[:, :, 0:1]
                    dve.did(nc.vector.memset(starts, 0.0))
            next_layer()
            driven_bank = [[psum[:, 2 * c + i, :] for i in range(2)] for c in range(NCH)]
            c_ring = Ring([psum[:, i, :] for i in (4, 5)])
            y_bank = [psum[:, 6 + c, :] for c in range(NCH)]
            pick_row = ct("pick_row", slice(0, 6 * DS))
            steps = [(g, n) for g in range(NGRP) for n in range(DS)]
            driven_free = [[None] * 2 for _ in range(NCH)]
            decay_free = [[None] * 2 for _ in range(NCH)]
            state_free = [[None] * 3 for _ in range(NCH)]
            c_row_free = [None] * 3
            y_free = [None] * NCH
            b_ready, decay_ready, c_ready, state_ready, y_done = {}, {}, {}, {}, {}

            def prepare(s):
                g, n = steps[s]
                cols, i = slice(BANK * g, BANK * g + BANK), s % 2
                for c in range(NCH):
                    pe.after(driven_free[c][i])
                    b_ready[s, c] = pe.did(nc.tensor.matmul(driven_bank[c][i], pick_row[:, P * n:P * n + P], rows16[:, cols],
                                                            start=True, stop=True))
                bank, free = c_ring.take()
                r = pe.did(pe.after(free).matmul(bank, pick_row[:, P * (DS + n):P * (DS + n) + P], rows16[:, cols], start=True, stop=True))
                for c in range(NCH):
                    live = decay[c][i].rearrange("p (s t) -> p s t", t=SEQ)[:, :, 1:SEQ]
                    seq = dt[:, c, cols].rearrange("p (s t) -> p s t", t=SEQ)[:, :, 1:SEQ]
                    act.after(decay_free[c][i])
                    decay_ready[s, c] = act.did(nc.scalar.activation(live, seq, ACT.Exp, scale=a_neg[:, DS * c + n:DS * c + n + 1]))
                act.after(r, c_row_free[s % 3])
                c_ready[s] = act.did(nc.scalar.activation(c_row[s % 3], bank, ACT.Copy))
                c_ring.release(bank, c_ready[s])

            def recur(s):
                g, n = steps[s]
                cols, i = slice(BANK * g, BANK * g + BANK), s % 2
                driven = []
                for c in range(NCH):
                    bank = driven_bank[c][i]
                    driven.append(dve.did(dve.after(b_ready[s, c]).tensor_tensor(bank, bank, dtu[:, c, cols], ALU.mult)))
                for c in range(NCH):
                    dve.after(driven[c], decay_ready[s, c], state_free[c][s % 3])
                    m = dve.did(nc.vector.tensor_tensor_scan(state[c][s % 3], decay[c][i], driven_bank[c][i], 0.0, ALU.mult, ALU.add))
                    state_ready[s, c] = driven_free[c][i] = decay_free[c][i] = m

            def read_out(s):
                for c in range(NCH):
                    pool.after(state_ready[s, c], c_ready[s])
                    y_done[s, c] = pool.did(nc.gpsimd.tensor_tensor(state[c][s % 3], state[c][s % 3], c_row[s % 3], ALU.mult))
                c_row_free[s % 3] = y_done[s, NCH - 1]

            marks = []

            def add_up(s):
                g, n = steps[s]
                cols = slice(BANK * g, BANK * g + BANK)
                for c in range(NCH):
                    pe.after(y_done[s, c], y_free[c])
                    state_free[c][s % 3] = pe.did(nc.tensor.matmul(y_bank[c], ident, state[c][s % 3], start=(n == 0), stop=(n == DS - 1)))
                if n < DS - 1:
                    return
                for c in range(NCH):
                    y_free[c] = dve.did(dve.after(state_free[c][s % 3]).scalar_tensor_tensor(
                        u[:, c, cols], u[:, c, cols], wt("d_b")[:, c:c + 1], y_bank[c], ALU.mult, ALU.add))
                y_ready = pool.did(pool.after(y_free).tensor_tensor(z[:, :, cols], z[:, :, cols], u[:, :, cols], ALU.mult))
                bank, free = c_ring.take()
                pe.after(free, y_ready)
                for q in range(GB):
                    j = GB * g + q
                    for c in range(NCH):
                        r = nc.tensor.matmul(bank[:, P * q:P * q + P], z[:, c, P * j:P * j + P], wt("out_b")[:, DM * c:DM * c + DM],
                                             start=(c == 0), stop=(c == NCH - 1))
                r = pe.did(r)
                added = dve.did(dve.after(r).tensor_tensor(x_cols[:, cols], x_cols[:, cols], bank, ALU.add))
                c_ring.release(bank, added)
                measure(g, added)

            for s in range(-1, len(steps) + 1):
                if s + 1 < len(steps):
                    prepare(s + 1)
                if 0 <= s < len(steps):
                    recur(s)
                    read_out(s)
                if s >= 1:
                    add_up(s - 1)

        state_space()
        next_layer(load_late.last(), zero_fill.last())
        experts(0)
        next_layer()
        selective_scan()
        next_layer()
        x_ready = experts(1)
        written = Transfers(sem("written"))
        for g in range(NGRP):
            cols = slice(BANK * g, BANK * g + BANK)
            written.sent(sp.after(x_ready[g]).dma_start(out[:, cols], x_cols[:, cols]))
        sp.after(written.last())


def constants():
    k, m = np.arange(P)[:, None], np.arange(P)[None, :]
    f = {
        "ident": k == m,
        "tri": np.concatenate([k <= m, np.ones((P, P))], 1),
        "shift": k == m + 1,
        "shift_in": (k == 0) & (m == P - 1),
        "inv_freq": (1.0 / 10000.0 ** (np.arange(HALF) / HALF) / (2 * np.pi))[None, :],
        "rev_expert": (NE - np.arange(NE))[None, :],
        "keep": np.tile(np.arange(NBLK) != 0, NE)[None, :],
        "slot": np.arange(NSLOT)[None, :],
    }
    row = np.arange(P)[:, None]
    mask = np.where(m < k, MASKED, 0.0)
    h = {
        "ident16": k == m,
        "tri16": k <= m,
        "ones16": np.ones((P, P)),
        "mask16": np.concatenate([mask, np.zeros((P, P)), mask], 1),
        "pick_head": (row < 3 * NH) & (row % NH == np.repeat(np.arange(NH), P)[None, :]),
        "pick_row": (row < 6 * DS) & (row % (2 * DS) == np.repeat(np.arange(2 * DS), P)[None, :]),
    }
    c16 = np.zeros((P, C_COLS), np.uint16)
    for name, value in h.items():
        at, width = C_AT[name]
        c16[:, at:at + width] = np.broadcast_to(value, (P, width)).astype(np.float32).view(np.uint32) >> 16
    return f, c16


def kernel(**inputs):
    import numpy as _np
    import concourse.bacc as _bacc
    from concourse import mybir as _mybir
    from concourse.bass_utils import run_bass_kernel_spmd as _run

    i = {name: _np.asarray(a) for name, a in inputs.items()}
    f32_consts, c16 = constants()

    def halves(a):
        return a.reshape(-1, P, a.shape[-1]).transpose(1, 0, 2).reshape(P, -1)

    wa = i["L0_attn_a_W_in"]
    z, xr, bm, cm, dtc = _np.split(wa, [256, 512, 768, 1024], axis=1)
    nr = 2 * DS + DR
    wx = _np.concatenate([i["L0_attn_b_W_x"][DR:nr], i["L0_attn_b_W_x"][0:DR]], 0).T
    packed = {
        "in_a": _np.concatenate([z, bm[:, 0::2], bm[:, 1::2], cm[:, 0::2], cm[:, 1::2], xr, dtc], 1),
        "dt_bias": i["L0_attn_a_dt_bias"][None, :],
        "a_log_a": i["L0_attn_a_A_log"][None, :],
        "norm_w": i["L0_attn_a_norm_weight"].reshape(NPAIR, P).T,
        "out_a": halves(i["L0_attn_a_W_out"]),
        "router": i["L0_ffn_router_w"].T,
        "shared_gate": i["L0_ffn_shared_gate_w"].T,
        "shared_up": i["L0_ffn_shared_up_w"].T,
        "shared_down": halves(i["L0_ffn_shared_down_w"].T),
        "gate_up": i["L0_ffn_gate_up_proj"].transpose(1, 0, 2).reshape(P, -1),
        "down": i["L0_ffn_down_proj"].transpose(1, 0, 2).reshape(P, -1),
        "in_b": i["L0_attn_b_W_in"].T,
        "conv_w": i["L0_attn_b_conv_w"].T.reshape(1, -1),
        "conv_b": i["L0_attn_b_conv_b"].reshape(NCH, P).T,
        "x_b": halves(wx),
        "dt_b": i["L0_attn_b_b_dt"].reshape(NCH, P).T,
        "a_log_b": halves(i["L0_attn_b_A_log"]),
        "d_b": i["L0_attn_b_D"].reshape(NCH, P).T,
        "out_b": halves(i["L0_attn_b_W_out"].T),
    }
    packed.update(f32_consts)
    w = _np.zeros((P, W_COLS), _np.float32)
    for name, value in packed.items():
        at, width = W_AT[name]
        w[:, at:at + width] = value
    at, width = W_AT["dt_w"]
    w[2 * DS:nr, at:at + width] = i["L0_attn_b_W_dt"].T
    x = i["L0_attn_a_hidden"].reshape(NBLK, P, DM).transpose(1, 0, 2).reshape(P, NBLK * DM)
    arrays = {"x_in": _np.ascontiguousarray(x), "w_in": w, "c_in": c16}

    nc = _bacc.Bacc("TRN2", target_bir_lowering=False, num_devices=1)
    args = [nc.dram_tensor(n, a.shape, _mybir.dt.from_np(a.dtype), kind="ExternalInput").ap() for n, a in arrays.items()]
    args.append(nc.dram_tensor("out_0", (P, NBLK * DM), _mybir.dt.float32, kind="ExternalOutput").ap())
    build(nc, *args)
    got = _run(nc, [arrays], core_ids=[0]).results[0]["out_0"]
    return got.reshape(P, NBLK, DM).transpose(1, 0, 2).reshape(BATCH, SEQ, DM)
```

```python
from contextlib import ExitStack

import numpy as np
import concourse.bass as bass
from concourse import mybir

F32, BF16, I32, U16 = mybir.dt.float32, mybir.dt.bfloat16, mybir.dt.int32, mybir.dt.uint16
ALU, ACT, AX = mybir.AluOpType, mybir.ActivationFunctionType, mybir.AxisListType

P = 128
BATCH, SEQ, DM = 8, 256, 128
NBLK = BATCH * SEQ // P
NTOK = BATCH * SEQ
BANK = 512
NGRP = NTOK // BANK
GB = BANK // P
NH, HD, NS = 4, 64, 64
HALF = NS // 2
NPAIR = NH * HD // P
FREQ_ROWS = 3 * 3 * NH
DECAY_AT, DECAY_END = 64, 64 + 3 * NH
NE, EF, SF = 16, 128, 512
NSC = SF // P
NSLOT = NBLK + NE - 1
ROW = DM + 1
FETCH = 8
EARLY = 3
PIECES = 5
DI, DS, DC, DR = 256, 16, 4, 8
NCH = DI // P
PARTS = 3
FULL_TURN = 6.283185
ROUND = 1.5 * 2.0 ** 23
LOG_EXP, SILU, TRIG = "natural_log_exp_and_others", "silu_and_others", "trig_and_small"
MASKED = -1e30

_W_EARLY = [("in_a", 1540), ("dt_bias", NH), ("a_log_a", NH), ("ident", P), ("tri", 2 * P), ("shift", P),
            ("shift_in", P), ("unfilled", NSLOT), ("norm_w", NPAIR), ("out_a", NPAIR * DM)]
_W_LATE = [("router", NE), ("shared_gate", SF), ("shared_up", SF), ("shared_down", NSC * DM),
           ("gate_up", NE * 2 * EF), ("down", NE * DM), ("rev_expert", NE), ("keep", NE * NBLK), ("slot", NSLOT), ("token", NBLK),
           ("in_b", 2 * DI), ("conv_w", DC * NCH), ("conv_b", NCH), ("x_b", NCH * (2 * DS + DR)), ("dt_w", DI),
           ("dt_b", NCH), ("a_log_b", NCH * DS), ("d_b", NCH), ("out_b", NCH * DM)]
_C16 = [("ident16", P), ("tri16", P), ("ones16", P), ("mask16", 2 * P), ("pick_head", NH * P), ("freq16", NH * NS),
        ("pick_row", 2 * DS * P)]


def offsets(table):
    at, found = 0, {}
    for name, width in table:
        found[name] = (at, width)
        at += width
    return found, at


W_AT, W_COLS = offsets(_W_EARLY + _W_LATE)
W_EARLY_COLS = offsets(_W_EARLY)[1]
C_AT, C_COLS = offsets(_C16)
C_EARLY_COLS = C_AT["pick_row"][0]


class Engine:

    def __init__(self, engine, semaphore):
        self.engine, self.semaphore, self.count, self.seen = engine, semaphore, 0, {}

    def after(self, *marks):
        for mark in marks:
            if isinstance(mark, list):
                self.after(*mark)
            elif mark is not None and self.seen.get(mark[0].name, 0) < mark[1]:
                self.engine.wait_ge(mark[0], mark[1])
                self.seen[mark[0].name] = mark[1]
        return self.engine

    def did(self, instruction):
        instruction.then_inc(self.semaphore, 1)
        self.count += 1
        return self.last()

    def last(self):
        return (self.semaphore, self.count)


class Transfers:

    def __init__(self, semaphore):
        self.semaphore, self.count = semaphore, 0

    def sent(self, dma):
        dma.then_inc(self.semaphore, 16)
        self.count += 16
        return (self.semaphore, self.count)

    def last(self):
        return (self.semaphore, self.count)


class Ring:

    def __init__(self, banks):
        self.banks, self.freed, self.turn, self.held = banks, [None] * len(banks), -1, set()

    def take(self):
        assert len(self.held) < len(self.banks)
        self.turn = (self.turn + 1) % len(self.banks)
        while self.turn in self.held:
            self.turn = (self.turn + 1) % len(self.banks)
        self.held.add(self.turn)
        return self.banks[self.turn], self.freed[self.turn]

    def release(self, bank, mark):
        self.held.remove(self.banks.index(bank))
        self.freed[self.banks.index(bank)] = mark


def build(nc, x_in, w_in, c_in, out):
    with ExitStack() as stack:
        def sb(name, shape, dtype=F32):
            return stack.enter_context(nc.sbuf_tensor(name, shape, dtype))

        def sem(name):
            return stack.enter_context(nc.semaphore(name))

        pe, dve = Engine(nc.tensor, sem("pe_done")), Engine(nc.vector, sem("dve_done"))
        act, pool = Engine(nc.scalar, sem("act_done")), Engine(nc.gpsimd, sem("pool_done"))
        sp = Engine(nc.sync, sem("sp_done"))

        psum = stack.enter_context(nc.psum_tensor("psum", [P, 8, BANK], F32))
        x = sb("x", [P, NBLK, DM])
        xn = sb("xn", [P, NBLK, DM])
        xnt = sb("xnt", [P, NTOK])
        logits = sb("logits", [P, NBLK * NE])
        w = sb("w", [P, W_COLS])
        c16 = sb("c16", [P, C_COLS], BF16)
        stats = sb("stats", [P, NBLK, 6])
        moments = sb("moments", [P, NBLK, 2])
        rstd = sb("rstd", [P, NBLK])
        consts = sb("consts", [P, 4])
        ARENA = 32256
        arena = sb("arena", [P, ARENA])
        sorted_x = [nc.dram_tensor(f"sorted_x{i}", [NSLOT * P, ROW], F32, kind="Internal").ap() for i in range(2)]
        result = [nc.dram_tensor(f"result{i}", [NTOK + NSLOT * P, DM], F32, kind="Internal").ap() for i in range(2)]

        def wt(name, rows=slice(0, P)):
            at, width = W_AT[name]
            return w[rows, at:at + width]

        def ct(name, rows=slice(0, P)):
            at, width = C_AT[name]
            return c16[rows, at:at + width]

        eps_ln, eps_rms, quarter_turn, one = (consts[:, i:i + 1] for i in range(4))
        ident, tri = wt("ident"), wt("tri")
        x_cols = x[:].rearrange("p b c -> p (b c)")

        def xnt_block(j):
            return xnt[:, P * j:P * j + P]

        def xnt_group(g):
            return xnt[:, BANK * g:BANK * g + BANK]

        SCAN_FIRST = 4 * NCH * NTOK + NTOK + 3 * BANK + BANK + NTOK // 2 + NCH * DS
        measured = [None] * NGRP

        def measure(g, ready):
            blocks = range(GB * g, GB * g + GB)
            dve.after(ready)
            for j in blocks:
                stat = dve.did(nc.vector.bn_stats(stats[:, j, :], x[:, j, :]))
            dve.after(stat)
            for j in blocks:
                measured[g] = dve.did(nc.vector.bn_aggr(moments[:, j, :], stats[:, j, :]))

        table = [None]

        def table_set(name):
            if table[0] != name:
                nc.scalar.preload_act_table_set(name)
                table[0] = name

        load_x = [Transfers(sem(f"load_x{g}")) for g in range(NGRP)]
        load_early, load_late, zero_fill = Transfers(sem("load_early")), Transfers(sem("load_late")), Transfers(sem("zero_fill"))
        for g in range(NGRP):
            cols = slice(BANK * g, BANK * g + BANK)
            load_x[g].sent(nc.sync.dma_start(x_cols[:, cols], x_in[:, cols]))
        load_early.sent(nc.scalar.dma_start(w[:, 0:W_EARLY_COLS], w_in[:, 0:W_EARLY_COLS]))
        load_early.sent(nc.scalar.dma_start(c16[:, 0:C_EARLY_COLS].bitcast(U16), c_in[:, 0:C_EARLY_COLS]))
        table_set(LOG_EXP)
        sp.after(load_early.last())
        load_late.sent(nc.sync.dma_start(w[:, W_EARLY_COLS:W_COLS], w_in[:, W_EARLY_COLS:W_COLS]))
        load_late.sent(nc.sync.dma_start(c16[:, C_EARLY_COLS:C_COLS].bitcast(U16), c_in[:, C_EARLY_COLS:C_COLS]))
        blank = arena[:, 2 * NPAIR * NTOK:2 * NPAIR * NTOK + NSLOT * ROW].rearrange("p (s c) -> p s c", s=NSLOT)
        pool.did(nc.gpsimd.memset(blank[:, :, 0:DM], 0.0))
        blanked = pool.did(pool.after(load_early.last()).tensor_copy(blank[:, :, DM:ROW], wt("unfilled").unsqueeze(2)))
        for buffer in sorted_x:
            zero_fill.sent(sp.after(blanked).dma_start(buffer.rearrange("(s p) c -> p s c", p=P), blank))
        for value, tile in ((1e-5, eps_ln), (1e-6, eps_rms), (float(np.pi / 2), quarter_turn), (1.0, one)):
            consts_set = pool.did(nc.gpsimd.memset(tile, value))
        for g in range(NGRP):
            measure(g, load_x[g].last())
        for e in (pe, dve, act, pool):
            e.after(load_early.last(), consts_set)

        def next_layer(*more):
            marks = [e.last() for e in (pe, dve, act, pool)] + list(more)
            for e in (pe, dve, act, pool):
                e.after(marks)

        def carve(first=0):
            taken = [first]

            def piece(columns, rows=slice(0, P)):
                taken[0] += columns
                assert taken[0] <= ARENA, taken
                return arena[rows, taken[0] - columns:taken[0]]
            return piece

        def inverse_root(target, source, eps, scale, ready):
            table_set(LOG_EXP)
            m = act.did(act.after(ready).activation(target, source, ACT.Ln, bias=eps, scale=scale))
            return act.did(act.after(m).activation(target, target, ACT.Exp, scale=-0.5))

        normed, routed = [None] * NGRP, [None] * NGRP

        def normalise(g, ring, route):
            blocks, cols = range(GB * g, GB * g + GB), slice(GB * g, GB * g + GB)
            mark = {}

            def root():
                mark["rstd"] = inverse_root(rstd[:, cols], moments[:, cols, 1], eps_ln, 1.0, measured[g])

            def scale():
                dve.after(mark["rstd"])
                for j in blocks:
                    mark["scaled"] = dve.did(nc.vector.tensor_scalar(xn[:, j, :], x[:, j, :], moments[:, j, 0:1],
                                                                     rstd[:, j:j + 1], ALU.subtract, ALU.mult))

            def turn():
                bank, free = ring.take()
                pe.after(mark["scaled"], free)
                for q, j in enumerate(blocks):
                    turned = pe.did(nc.tensor.transpose(bank[:, P * q:P * q + P], xn[:, j, :], ident))
                normed[g] = act.did(act.after(turned).activation(xnt_group(g), bank, ACT.Copy))
                ring.release(bank, normed[g])

            def logits_of():
                bank, free = ring.take()
                pe.after(normed[g], free)
                for q, j in enumerate(blocks):
                    r = nc.tensor.matmul(bank[:, NE * q:NE * q + NE], xnt_block(j), wt("router"), start=True, stop=True)
                r = pe.did(r)
                routed[g] = dve.did(dve.after(r).tensor_copy(logits[:, NE * GB * g:NE * GB * (g + 1)], bank[:, 0:NE * GB]))
                ring.release(bank, routed[g])
            return [root, scale, turn] + ([logits_of] if route else [])

        def normalise_all(ring, route):
            for steps in zip(*[normalise(g, ring, route) for g in range(NGRP)]):
                for step in steps:
                    step()

        def state_space():
            piece = carve()
            z_silu = piece(NPAIR * NTOK).rearrange("p (c t) -> p c t", c=NPAIR)
            xw = piece(NBLK * NH * HD).rearrange("p (j h c) -> p j h c", j=NBLK, h=NH)
            rotated = [[piece(NTOK) for _ in range(NH // 2)] for _ in range(2)]
            cosine, sine = ([piece(NTOK) for _ in range(NH // 2)] for _ in range(2))
            dt = piece(NBLK * NH)
            small = [piece(NBLK * NH) for _ in range(8)]
            cum = piece(NBLK * NH)
            neg_cum, neg_u = piece(NBLK * NH), piece(NBLK * NH)
            a_row = piece(NH)
            parts = piece(NBLK * P // 2).bitcast(BF16).rearrange("p (j r) -> p j r", j=NBLK)
            sum_rows = piece(NTOK // 2, slice(0, P)).bitcast(BF16)
            products = [piece(BANK) for _ in range(2)]
            decay = [piece(3 * P) for _ in range(4)]
            mixed = [piece(3 * P) for _ in range(3)]
            out_w = piece(NPAIR * DM)
            squares = piece(NPAIR * SEQ).rearrange("p (c t) -> p c t", c=NPAIR)
            inverse_rms = piece(NBLK)
            n4 = NBLK * NH

            ring = Ring([psum[:, i, :] for i in (0, 1, 4, 5, 6, 7)])
            normalise_all(ring, False)
            in_a = wt("in_a")
            z_w, bc_w = in_a[:, 0:2 * P], in_a[:, 2 * P:10 * P]
            xr_w, dt_w = in_a[:, 10 * P:12 * P], in_a[:, 12 * P:12 * P + NH]

            def project_z(g):
                cols = slice(BANK * g, BANK * g + BANK)
                for c in range(NPAIR):
                    bank, free = ring.take()
                    r = pe.did(pe.after(free).matmul(bank, z_w[:, P * c:P * c + P], xnt_group(g), start=True, stop=True))
                    ring.release(bank, act.did(act.after(r).activation(z_silu[:, c, cols], bank, ACT.Silu)))

            dt_bank, aux_bank = psum[:, 2, 0:n4], psum[:, 3, :]
            for j in range(NBLK):
                pe.after(normed[j // GB])
                raw_ready = pe.did(nc.tensor.matmul(dt_bank[:, NH * j:NH * j + NH], xnt_block(j), dt_w, start=True, stop=True))
            v, least, e, log1p, shifted, total, inverse, half = small

            def heads(t):
                return t.rearrange("p (j h) -> p j h", h=NH)

            def per_head(row):
                return row.unsqueeze(1).to_broadcast([P, NBLK, NH])

            m = dve.did(dve.after(raw_ready).tensor_tensor(heads(v), heads(dt_bank), per_head(wt("dt_bias")), ALU.add))
            m = dve.did(dve.after(m).scalar_tensor_tensor(least, v, -1.0, v, ALU.mult, ALU.min))
            table_set(LOG_EXP)
            e_ready = act.did(act.after(m).activation(e, least, ACT.Exp))
            a_exp = act.did(nc.scalar.activation(a_row, wt("a_log_a"), ACT.Exp))
            log_ready = act.did(act.after(e_ready).activation(log1p, e, ACT.Ln, bias=one))
            table_set(TRIG)
            dt_ready = dve.did(dve.after(log_ready).scalar_tensor_tensor(dt, v, 0.0, log1p, ALU.max, ALU.add))
            rows_ready = [None, None]
            nc.gpsimd.memset(parts[:, :, FREQ_ROWS:DECAY_AT], 0.0)
            gap_set = pool.did(nc.gpsimd.memset(parts[:, :, DECAY_END:P], 0.0))
            neg_dta = half
            m = dve.did(dve.after(a_exp, dt_ready).tensor_tensor(heads(neg_dta), heads(dt), per_head(a_row), ALU.mult))
            sum_dt = psum[:, 2, n4:2 * n4]
            pe.after(dt_ready)
            nc.tensor.matmul(sum_dt, tri[:, 0:P], dt, start=True, stop=True, skip_group_check=True)
            summed = pe.did(nc.tensor.matmul(heads(sum_dt)[:, 1::2, :], tri[:, P:2 * P], heads(dt)[:, 0::2, :],
                                             start=False, stop=True, skip_group_check=True))
            pe.after(m)
            nxt, run = aux_bank[:, 0:n4], aux_bank[:, n4:2 * n4]
            odd_dt, even_cols = heads(dt)[:, 1::2, :], heads(nxt)[:, 0::2, :]
            nc.tensor.matmul(nxt, wt("shift"), dt, start=True, stop=True)
            nc.tensor.matmul(even_cols, wt("shift_in"), odd_dt, start=False, stop=True, skip_group_check=True)
            nc.tensor.matmul(run, tri[:, 0:P], neg_dta, start=False, stop=True, skip_group_check=True)
            sums = pe.did(nc.tensor.matmul(heads(run)[:, 1::2, :], tri[:, P:2 * P], heads(neg_dta)[:, 0::2, :],
                                           start=False, stop=True, skip_group_check=True))
            def split(source, columns, copies, ready):
                at, shape = columns.start, [P, NBLK, copies, NH]
                target = [parts[:, :, at + copies * NH * i:at + copies * NH * (i + 1)].rearrange("p j (k h) -> p j k h", h=NH)
                          for i in range(PARTS)]

                def spread(t):
                    return heads(t).unsqueeze(2).to_broadcast(shape)
                m = dve.did(dve.after(ready).tensor_copy(target[0], spread(source)))
                m = dve.did(dve.after(m).tensor_tensor(heads(rest), heads(source), target[0][:, :, 0, :], ALU.subtract))
                m = dve.did(dve.after(m).tensor_copy(target[1], spread(rest)))
                return dve.did(dve.after(m).tensor_tensor(target[2], spread(rest), target[1], ALU.subtract))

            rest = log1p
            split(sum_dt, slice(0, FREQ_ROWS), PARTS, [summed, gap_set])
            dve.after(sums)
            dve.did(nc.vector.tensor_copy(neg_cum, run))
            m_cum = dve.did(nc.vector.tensor_scalar(cum, run, -1.0, None, ALU.mult))
            m4 = split(cum, slice(DECAY_AT, DECAY_END), 1, [m_cum, gap_set])
            pe.after(m4)
            for k in range(2):
                bank, free = ring.take()
                pe.after(free)
                rows = bank.bitcast(BF16)[0:P, :]
                for j in range(8):
                    turned = pe.did(nc.tensor.transpose(rows[:, P * j:P * j + P], parts[:, 8 * k + j, :], ct("ident16")))
                rows_ready[k] = act.did(act.after(turned).activation(sum_rows[:, 8 * P * k:8 * P * k + 8 * P], rows, ACT.Copy))
                ring.release(bank, rows_ready[k])
            m_shift = dve.did(nc.vector.tensor_copy(shifted, nxt))
            m_tot = dve.did(dve.after(m_shift).tensor_tensor(total, dt, shifted, ALU.add))
            weight_ready = dve.did(dve.after(m_tot).tensor_scalar(v, total, 0.5, None, ALU.mult))
            m = dve.did(nc.vector.tensor_scalar(e, total, 1e-30, None, ALU.max))
            m = dve.did(dve.after(m).reciprocal(inverse, e))
            dve.did(dve.after(m).scalar_tensor_tensor(neg_u, shifted, -1.0, inverse, ALU.mult, ALU.mult))

            trig = {}

            def angles(g, q):
                bank, free = ring.take()
                cols = slice(BANK * g, BANK * g + BANK)
                r = pe.did(pe.after(free, rows_ready[g // 2]).matmul(
                    bank, ct("freq16", slice(0, FREQ_ROWS))[:, P * q:P * q + P], sum_rows[0:FREQ_ROWS, cols], start=True, stop=True))
                i = turn_count[0] % 2
                turn_count[0] += 1
                co, si, whole = cosine[q][:, cols], sine[q][:, cols], products[i]
                m = dve.did(dve.after(r, product_free[i]).tensor_scalar(whole, bank, ROUND, None, ALU.add))
                m = dve.did(dve.after(m).scalar_tensor_tensor(si, whole, ROUND, bank, ALU.subtract, ALU.subtract))
                product_free[i] = m
                ring.release(bank, m)
                table_set(TRIG)
                m = act.did(act.after(m).activation(co, si, ACT.Abs))
                nc.scalar.activation(si, si, ACT.Sin, scale=-FULL_TURN)
                trig[g, q] = act.did(act.after(m).activation(co, co, ACT.Sin, scale=-FULL_TURN, bias=quarter_turn))

            def weigh(g):
                for j in range(GB * g, GB * g + GB, 2):
                    bank, free = ring.take()
                    pe.after(free)
                    for i in range(2):
                        r = pe.did(nc.tensor.matmul(bank[:, 2 * P * i:2 * P * i + 2 * P], xnt_block(j + i), xr_w, start=True, stop=True))
                    xw_ready = dve.did(dve.after(r, weight_ready).tensor_tensor(
                        xw[:, j:j + 2, :, :].rearrange("p j h c -> p (j h) c"), bank.rearrange("p (q c) -> p q c", c=HD),
                        v[:, NH * j:NH * j + 2 * NH].unsqueeze(2).to_broadcast([P, 2 * NH, HD]), ALU.mult))
                    ring.release(bank, xw_ready)

            product_free = [None] * 2
            rotated_ready = {}
            turn_count = [0]

            def rotate(g, k, q, banks):
                cols = slice(BANK * g, BANK * g + BANK)
                i = turn_count[0] % 2
                turn_count[0] += 1
                target, bank_of = rotated[k][q][:, cols], []
                for partner in range(2):
                    bank, free = banks.take()
                    at = P * (4 * k + 2 * partner + q)
                    bank_of.append((bank, pe.did(pe.after(free).matmul(bank, bc_w[:, at:at + P], xnt_group(g), start=True, stop=True))))
                (bank, r), (bank_p, r_p) = bank_of
                m = dve.did(dve.after(r, trig[g, q]).tensor_tensor(target, bank, cosine[q][:, cols], ALU.mult))
                banks.release(bank, m)
                m = dve.did(dve.after(r_p, product_free[i]).tensor_tensor(products[i], bank_p, sine[q][:, cols], ALU.mult))
                banks.release(bank_p, m)
                rotated_ready[g, k, q] = product_free[i] = pool.did(pool.after(m).tensor_tensor(target, target, products[i], ALU.add))

            for g in range(2):
                for q in range(NH // 2):
                    angles(g, q)
            dve.after(zero_fill.last())
            for q in range(NH // 2):
                for k in range(2):
                    rotate(0, k, q, ring)
                weigh(q)
                for p in range(NH // 2):
                    angles(2 + q, p)
            for g in range(2, NGRP):
                weigh(g)
            table_set(SILU)
            for g in range(NGRP):
                project_z(g)
            table_set(LOG_EXP)
            for c in range(NPAIR):
                w_ready = dve.did(nc.vector.tensor_scalar(out_w[:, DM * c:DM * c + DM], wt("out_a")[:, DM * c:DM * c + DM],
                                                          wt("norm_w")[:, c:c + 1], None, ALU.mult))

            next_layer(load_late.last())
            exponents = Ring([psum[:, i, :] for i in (0, 1)])
            scores = Ring([psum[:, i, :] for i in (2, 3)])
            outputs = Ring([psum[:, i, :] for i in (4, 5)])
            others = Ring([psum[:, i, :] for i in (6, 7)])
            units = [(b, h) for b in range(BATCH) for h in range(NH)]
            decay_ready, decay_free = [None] * len(units), [None] * len(decay)
            mixed_ready, mixed_free = [None] * len(units), [None] * len(mixed)

            def decays(i):
                b, h = units[i]
                bank, free = exponents.take()
                pe.after(free)
                pick, sums = ct("pick_head")[:, P * h:P * h + P], sum_rows
                t0, tm, t1 = SEQ * b, SEQ * b + P, SEQ * b + SEQ
                nc.tensor.matmul(bank[:, 0:2 * P], pick, sums[:, t0:t1], start=True, stop=True, skip_group_check=True)
                nc.tensor.matmul(bank[:, 2 * P:3 * P], pick, sums[:, tm:t1], start=False, stop=True, skip_group_check=True)
                diagonal_blocks = bank.rearrange("p (q k) -> p q k", q=2)[:, :, 0:P]
                exponent = pe.did(nc.tensor.matmul(diagonal_blocks, ct("ident16"), ct("mask16"), start=False, stop=True,
                                                   skip_group_check=True))
                k = i % len(decay)
                d, j = decay[k], 2 * b
                act.after(exponent, decay_free[k])
                table_set(LOG_EXP)
                nc.scalar.activation(d[:, 0:2 * P], bank[:, 0:2 * P], ACT.Exp, bias=neg_cum[:, NH * j + h:NH * j + h + 1])
                decayed = act.did(nc.scalar.activation(d[:, 2 * P:3 * P], bank[:, 2 * P:3 * P], ACT.Exp,
                                                       bias=neg_cum[:, NH * (j + 1) + h:NH * (j + 1) + h + 1]))
                exponents.release(bank, decayed)
                dve.after(decayed)
                for q, cols in ((0, slice(0, P)), (1, slice(2 * P, 3 * P))):
                    decay_ready[i] = dve.did(nc.vector.scalar_tensor_tensor(
                        d[:, cols], ident, neg_u[:, NH * (j + q) + h:NH * (j + q) + h + 1], d[:, cols], ALU.mult, ALU.add))

            def score(i):
                b, h = units[i]
                q, rows = h // 2, slice(NS * (h % 2), NS * (h % 2) + NS)
                t0, tm, t1 = SEQ * b, SEQ * b + P, SEQ * b + SEQ
                bank, free = scores.take()
                pe.after(free, rotated_ready[b // 2, 0, q], rotated_ready[b // 2, 1, q])
                b_rows, c_rows = rotated[0][q][rows, :], rotated[1][q][rows, :]
                nc.tensor.matmul(bank[:, 0:2 * P], b_rows[:, t0:tm], c_rows[:, t0:t1], start=True, stop=True, skip_group_check=True)
                scored = nc.tensor.matmul(bank[:, 2 * P:3 * P], b_rows[:, tm:t1], c_rows[:, tm:t1], start=False, stop=True,
                                          skip_group_check=True)
                scored = pe.did(scored)
                k = i % len(mixed)
                dve.after(scored, decay_ready[i], mixed_free[k])
                mixed_ready[i] = dve.did(nc.vector.tensor_tensor(mixed[k], bank[:, 0:3 * P], decay[i % len(decay)], ALU.mult))
                scores.release(bank, mixed_ready[i])
                decay_free[i % len(decay)] = mixed_ready[i]

            y_bank = [None, None]

            def output(i):
                b, h = units[i]
                if h == 0:
                    y_bank[0], y_bank[1] = outputs.take()
                bank = y_bank[0]
                pe.after(mixed_ready[i], y_bank[1])
                rows, at = slice(HD * (h % 2), HD * (h % 2) + HD), SEQ * (h // 2)
                g = mixed[i % len(mixed)]
                nc.tensor.matmul(bank[rows, at:at + SEQ], xw[:, 2 * b, h, :], g[:, 0:2 * P], start=True, stop=True,
                                 skip_group_check=True)
                m = pe.did(nc.tensor.matmul(bank[rows, at + P:at + SEQ], xw[:, 2 * b + 1, h, :], g[:, 2 * P:3 * P],
                                            start=False, stop=True, skip_group_check=True))
                mixed_free[i % len(mixed)] = m
                if h == NH - 1:
                    gate = z_silu[:, :, SEQ * b:SEQ * b + SEQ]
                    gated = dve.did(dve.after(m).tensor_tensor(gate, bank.rearrange("p (c t) -> p c t", c=NPAIR), gate, ALU.mult))
                    outputs.release(bank, gated)
                    gated_of[b] = gated

            gated_of, squares_free = {}, {"mark": None}

            def finish(b):
                cols, mark = slice(SEQ * b, SEQ * b + SEQ), {}
                blocks = (2 * b, 2 * b + 1)

                def square():
                    mark["square"] = act.did(act.after(gated_of[b], squares_free["mark"]).activation(squares, z_silu[:, :, cols], ACT.Square))

                def project_out():
                    bank, free = others.take()
                    pe.after(free, gated_of[b], w_ready)
                    pe.after(mark["square"])
                    for i, j in enumerate(blocks):
                        for c in range(NPAIR):
                            r = nc.tensor.matmul(bank[:, 2 * P + i:2 * P + i + 1], squares[:, c, P * i:P * i + P], tri[:, P:P + 1],
                                                 start=(i == 0 and c == 0), stop=True, skip_group_check=True)
                    squares_free["mark"] = pe.did(r)
                    for i, j in enumerate(blocks):
                        for c in range(NPAIR):
                            r = nc.tensor.matmul(bank[:, P * i:P * i + P], z_silu[:, c, P * j:P * j + P], out_w[:, DM * c:DM * c + DM],
                                                 start=False, stop=True, skip_group_check=True)
                    mark["out"] = pe.did(r)
                    mark["bank"] = bank

                def root():
                    mark["rms"] = inverse_root(inverse_rms[:, 2 * b:2 * b + 2], mark["bank"][:, 2 * P:2 * P + 2], eps_rms,
                                               1.0 / (NH * HD), mark["out"])

                def add():
                    dve.after(mark["rms"])
                    for i, j in enumerate(blocks):
                        added = dve.did(nc.vector.scalar_tensor_tensor(
                            x[:, j, :], mark["bank"][:, P * i:P * i + P], inverse_rms[:, j:j + 1], x[:, j, :], ALU.mult, ALU.add))
                    others.release(mark["bank"], added)
                    if b % 2 == 1:
                        measure(b // 2, added)
                return [square, project_out, root, add] + (normalise(b // 2, others, True) if b % 2 == 1 else [])

            later, ahead = [], 2
            for g in range(1, NGRP):
                for n, (q, k) in enumerate([(q, k) for q in range(NH // 2) for k in range(2)]):
                    later.append((2 * NH * (g - 1) + (0, 1, NH, NH + 1)[n], lambda g=g, k=k, q=q: rotate(g, k, q, others)))
            for i in range(-ahead, len(units) + 1):
                if 0 <= i < len(units):
                    score(i)
                if i + ahead < len(units):
                    decays(i + ahead)
                if i >= 1:
                    output(i - 1)
                while later and later[0][0] <= i:
                    later.pop(0)[1]()
                if i >= 1:
                    if units[i - 1][1] == NH - 1:
                        square, *rest_of = finish(units[i - 1][0])
                        square()
                        later += [(i + due, work) for due, work in zip((2, 3, 3, 4, 5, 6, 7), rest_of)]
                        later.sort(key=lambda item: item[0])
            return [work for _, work in later], 0, (exponents, scores, outputs, others)

        def experts(turn, pending, projection, rings):
            piece = carve()
            xs_rows = piece(NSLOT * ROW).rearrange("p (s c) -> p s c", s=NSLOT)
            xs_t = piece(NSLOT * P)
            y_rows = piece(NSLOT * DM).rearrange("p (s c) -> p s c", s=NSLOT)
            scaled = piece(NBLK * ROW).rearrange("p (j c) -> p j c", j=NBLK)
            result_row = piece(NSLOT).bitcast(I32)
            logit_max, best, score = (piece(NBLK) for _ in range(3))
            chosen, running, base, rank = (piece(NBLK * NE) for _ in range(4))
            one_hot16 = piece(NBLK * NE // 2).bitcast(BF16)
            n_slots, end_slot, n_rows, start_row = (piece(NE) for _ in range(4))
            passed = piece(NSLOT * NE)
            expert = piece(NSLOT)
            expert_int = piece(NSLOT).bitcast(I32)
            shared_act = [piece(NSC * BANK).rearrange("p (c t) -> p c t", c=NSC) for _ in range(2)]
            shared_gate = [piece(BANK) for _ in range(2)]
            piece = carve(SCAN_FIRST)
            position = piece(NBLK)
            position_int = piece(NBLK).bitcast(I32)
            gathered = piece(NBLK * DM).rearrange("p (j c) -> p j c", j=NBLK)
            gate = [piece(2 * EF) for _ in range(2)]
            hidden = [piece(2 * EF) for _ in range(3)]
            hidden_t = [piece(2 * EF) for _ in range(2)]

            def by_token(t):
                return t.rearrange("p (j n) -> p j n", n=NE)

            def by_expert(t):
                return t.rearrange("p (n j) -> p j n", j=NBLK)

            marks = {}

            def route():
                for i, work in enumerate(pending):
                    if i == projection:
                        shared_projections(0, 0)
                    work()
                m_max = dve.did(dve.after(routed).tensor_reduce(logit_max, by_token(logits[:]), AX.X, ALU.max))
                table_set(LOG_EXP)
                m_exp = act.did(act.after(m_max).activation(score, logit_max, ACT.Exp, scale=-1.0))
                yield
                m = dve.did(dve.after(m_max).tensor_tensor(
                    by_token(chosen), by_token(logits[:]), logit_max.unsqueeze(2).to_broadcast([P, NBLK, NE]), ALU.is_equal))
                rev = wt("rev_expert").unsqueeze(1).to_broadcast([P, NBLK, NE])
                yield
                m = dve.did(dve.after(m).tensor_tensor(by_token(rank), by_token(chosen), rev, ALU.mult))
                yield
                m = dve.did(dve.after(m).tensor_reduce(best, by_token(rank), AX.X, ALU.max))
                yield
                m_hot16 = dve.did(dve.after(m).tensor_tensor(
                    by_expert(one_hot16), rev, best.unsqueeze(2).to_broadcast([P, NBLK, NE]), ALU.is_equal))
                yield
                m_exp = dve.did(dve.after(m_exp).tensor_scalar(score, score, 1.0, 3e38, ALU.add, ALU.min))
                yield
                scored = dve.did(dve.after(m_exp).reciprocal(score, score))
                yield
                pe.after(m_hot16)
                (in_block_bank, free), (total_bank, free_too) = count_ring.take(), count_ring.take()
                in_block, block_total = in_block_bank[:, 0:NBLK * NE], total_bank[:, 0:NBLK * NE]
                pe.after(free, free_too)
                nc.tensor.matmul(in_block, ct("tri16"), one_hot16, start=True, stop=True)
                r = pe.did(nc.tensor.matmul(block_total, ct("ones16"), one_hot16, start=True, stop=True))
                marks["scaled"] = pool.did(pool.after(scored).tensor_tensor(
                    scaled[:, :, 0:DM], xn[:], score.unsqueeze(2).to_broadcast([P, NBLK, DM]), ALU.mult))
                yield
                m_run = dve.did(dve.after(r).tensor_tensor_scan(running, wt("keep"), block_total, 0.0, ALU.mult, ALU.add))
                counts = running.rearrange("p (n j) -> p n j", j=NBLK)[:, :, NBLK - 1]
                yield
                m = dve.did(dve.after(m_run).tensor_scalar(n_slots, counts, 1.0 / P, (P - 1.0) / P - (P - 1.0) / (2 * P), ALU.mult, ALU.add))
                yield
                m_slots = dve.did(dve.after(m).tensor_scalar(n_slots, n_slots, ROUND, -ROUND, ALU.add, ALU.add))
                yield
                m_end = dve.did(dve.after(m_slots).tensor_tensor_scan(end_slot, tri[:, P:P + NE], n_slots, 0.0, ALU.mult, ALU.add))
                m_before = dve.did(nc.vector.tensor_scalar(n_rows, n_slots, float(P), 1.0, ALU.mult, ALU.add))
                m_base = dve.did(nc.vector.tensor_tensor(base, running, block_total, ALU.subtract))
                in_rank = rank.rearrange("p (n j) -> p n j", j=NBLK)
                yield
                m_start = dve.did(dve.after(m_end, m_before).scalar_tensor_tensor(start_row, end_slot, float(P), n_rows, ALU.mult, ALU.subtract))
                m_rank = dve.did(dve.after(m_base).tensor_tensor(rank, in_block, base, ALU.add))
                for bank in (in_block_bank, total_bank):
                    count_ring.release(bank, m_rank)
                yield
                m = dve.did(dve.after(m_start, m_rank).tensor_tensor(
                    in_rank, in_rank, start_row.unsqueeze(2).to_broadcast([P, NE, NBLK]), ALU.add))
                yield
                m = dve.did(dve.after(m).tensor_tensor(rank, rank, one_hot16, ALU.mult))
                yield
                m = dve.did(dve.after(m).tensor_reduce(position, by_expert(rank), AX.X, ALU.add))
                yield
                marks["placed"] = dve.did(dve.after(m).tensor_copy(position_int, position))
                yield
                m = dve.did(dve.after(m_end).tensor_tensor(
                    passed.rearrange("p (s n) -> p s n", n=NE), wt("slot").unsqueeze(2).to_broadcast([P, NSLOT, NE]),
                    end_slot.unsqueeze(1).to_broadcast([P, NSLOT, NE]), ALU.is_ge))
                yield
                m = dve.did(dve.after(m).tensor_reduce(expert, passed.rearrange("p (s n) -> p s n", n=NE), AX.X, ALU.add))
                yield
                m = dve.did(dve.after(m).tensor_scalar(expert, expert, float(NE - 1), None, ALU.min))
                yield
                marks["expert"] = dve.did(dve.after(m).tensor_copy(expert_int, expert))

                pool.after(marks["placed"], marks["scaled"], numbered, zero_fill.last())
                for j in range(NBLK):
                    scatter.sent(nc.gpsimd.indirect_dma_start(
                        sorted_x[turn], bass.IndirectOffsetOnAxis(position_int[:, j:j + 1], 0), scaled[:, j, :], None))
                rows = sorted_x[turn].rearrange("(s p) c -> p s c", p=P)
                for i, transfer in enumerate(fetch):
                    slots = slice(FETCH * i, min(FETCH * i + FETCH, NSLOT))
                    transfer.sent(sp.after(scatter.last()).dma_start(xs_rows[:, slots, :], rows[:, slots, :]))

            scatter, put_back = Transfers(sem(f"scatter{turn}")), Transfers(sem(f"put_back{turn}"))
            fetch = [Transfers(sem(f"fetch{turn}_{i}")) for i in range(-(-NSLOT // FETCH))]
            read_back = [Transfers(sem(f"read_back{turn}_{g}")) for g in range(NGRP)]
            for e in (dve, act, pool):
                e.after([other.last() for other in (pe, dve, act, pool)])
            numbered = pool.did(nc.gpsimd.tensor_copy(scaled[:, :, DM:ROW], wt("token").unsqueeze(2)))
            routing = route()

            up_ring, gate_ring, down_ring, count_ring = rings
            shared_added = [None] * NGRP
            down_done = [None] * NGRP
            gate_free = [None, None]

            def shared_down(g):
                bank, free = down_ring.take()
                pe.after(free, hidden_ready[g])
                for q in range(GB):
                    for c in range(NSC):
                        r = nc.tensor.matmul(bank[:, P * q:P * q + P], shared_act[g % 2][:, c, P * q:P * q + P],
                                             wt("shared_down")[:, DM * c:DM * c + DM], start=(c == 0), stop=(c == NSC - 1))
                down_done[g] = pe.did(r)
                cols = x_cols[:, BANK * g:BANK * g + BANK]
                shared_added[g] = dve.did(dve.after(down_done[g]).tensor_tensor(cols, bank, cols, ALU.add))
                down_ring.release(bank, shared_added[g])

            hidden_ready = [None] * NGRP
            projected = {}

            def shared_projections(g, c):
                cols, found = slice(P * c, P * c + P), []
                for ring, weights in ((gate_ring, wt("shared_gate")), (up_ring, wt("shared_up"))):
                    bank, free = ring.take()
                    pe.after(free, normed[g])
                    found += [bank, pe.did(nc.tensor.matmul(bank, weights[:, cols], xnt_group(g), start=True, stop=True))]
                projected[g, c] = found

            def shared_up_gate(g):
                for c in range(NSC):
                    if (g, c) not in projected:
                        shared_projections(g, c)
                    bank_g, r_g, bank_u, r_u = projected[g, c]
                    sg = shared_gate[c % 2]
                    table_set(SILU)
                    m = act.did(act.after(r_g, gate_free[c % 2]).activation(sg, bank_g, ACT.Silu))
                    gate_ring.release(bank_g, m)
                    dve.after(r_u, m, down_done[g - 2] if g >= 2 else None)
                    hidden_ready[g] = dve.did(nc.vector.tensor_tensor(shared_act[g % 2][:, c, :], bank_u, sg, ALU.mult))
                    gate_free[c % 2] = hidden_ready[g]
                    up_ring.release(bank_u, hidden_ready[g])
                    for _ in range(PIECES):
                        next(routing, None)

            next(routing)
            for g in range(EARLY):
                shared_up_gate(g)
                if g >= 1:
                    shared_down(g - 1)
            shared_down(EARLY - 1)

            for _ in routing:
                pass
            next_layer()
            turn_ring = Ring([psum[:, i, :] for i in (0, 1)])
            up_ring = Ring([psum[:, i, :] for i in (2, 3)])
            flip_ring = Ring([psum[:, i, :] for i in (4, 5)])
            down_ring = Ring([psum[:, i, :] for i in (6, 7)])
            pairs = [tuple(range(s, min(s + 2, NSLOT))) for s in range(0, NSLOT, 2)]
            gate_up, down = wt("gate_up"), wt("down")
            turned_in, row_known = [None] * NSLOT, [None] * NSLOT
            hidden_free, gate_used, flipped_free = [None] * 3, [None] * 2, [None] * 2
            chosen_expert, hidden_done, flipped = {}, {}, {}

            def turn_in(s0):
                slots = range(s0, min(s0 + GB, NSLOT))
                n, arrived = len(slots), fetch[s0 // FETCH].last()
                bank, free = turn_ring.take()
                pe.after(free, arrived)
                for q, s in enumerate(slots):
                    r = nc.tensor.transpose(bank[:, P * q:P * q + P], xs_rows[:, s, 0:DM], ident)
                r = pe.did(r)
                m = act.did(act.after(r).activation(xs_t[:, P * s0:P * s0 + P * n], bank[:, 0:P * n], ACT.Copy))
                turn_ring.release(bank, m)
                known = dve.did(dve.after(arrived).tensor_copy(result_row[:, s0:s0 + n].unsqueeze(2), xs_rows[:, s0:s0 + n, DM:ROW]))
                for s in slots:
                    turned_in[s], row_known[s] = m, known

            def expand(k):
                bank, free = up_ring.take()
                n = len(pairs[k])
                pe.after(free, [turned_in[s] for s in pairs[k]], marks["expert"])
                for q, s in enumerate(pairs[k]):
                    chosen_expert[s] = nc.tensor.value_load(expert_int[0:1, s:s + 1], min_val=0, max_val=NE - 1)
                    r = nc.tensor.matmul(bank[:, 2 * EF * q:2 * EF * q + 2 * EF], xs_t[:, P * s:P * s + P],
                                         gate_up[:, bass.ds(chosen_expert[s] * (2 * EF), 2 * EF)], start=True, stop=True)
                r = pe.did(r)
                halves = bank.rearrange("p (q u f) -> p q u f", q=2, u=2)
                table_set(SILU)
                gt = gate[k % 2].rearrange("p (q f) -> p q f", q=2)[:, 0:n, :]
                m = act.did(act.after(r, gate_used[k % 2]).activation(gt, halves[:, 0:n, 0, :], ACT.Silu))
                hd = hidden[k % 3].rearrange("p (q f) -> p q f", q=2)[:, 0:n, :]
                m = dve.did(dve.after(m, hidden_free[k % 3]).tensor_tensor(hd, halves[:, 0:n, 1, :], gt, ALU.mult))
                gate_used[k % 2] = hidden_done[k] = m
                up_ring.release(bank, m)

            def flip(k):
                bank, free = flip_ring.take()
                pe.after(free, hidden_done[k])
                n = len(pairs[k])
                for q in range(n):
                    r = nc.tensor.transpose(bank[:, P * q:P * q + P], hidden[k % 3][:, EF * q:EF * q + EF], ident)
                hidden_free[k % 3] = pe.did(r)
                m = dve.did(dve.after(hidden_free[k % 3], flipped_free[k % 2]).tensor_copy(hidden_t[k % 2][:, 0:P * n], bank[:, 0:P * n]))
                flip_ring.release(bank, m)
                flipped[k] = m

            def contract(k):
                bank, free = down_ring.take()
                pe.after(free, flipped[k])
                for q, s in enumerate(pairs[k]):
                    r = nc.tensor.matmul(bank[:, P * q:P * q + P], hidden_t[k % 2][:, P * q:P * q + P],
                                         down[:, bass.ds(chosen_expert[s] * DM, DM)], start=True, stop=True)
                flipped_free[k % 2] = pe.did(r)
                n, s0 = len(pairs[k]), pairs[k][0]
                m = act.did(act.after(flipped_free[k % 2]).activation(
                    y_rows[:, s0:s0 + n, :], bank[:, 0:P * n].rearrange("p (q c) -> p q c", q=n), ACT.Copy))
                down_ring.release(bank, m)
                for s in pairs[k]:
                    pool.after(m, row_known[s])
                    put_back.sent(nc.gpsimd.indirect_dma_start(
                        result[turn], bass.IndirectOffsetOnAxis(result_row[:, s:s + 1], 0), y_rows[:, s, :], None))

            turn_in(0)
            for k in range(len(pairs) + 2):
                if k % 2 == 0 and 2 * k + GB < NSLOT:
                    turn_in(2 * k + GB)
                if k < len(pairs):
                    expand(k)
                if k >= 2:
                    contract(k - 2)
                if 1 <= k <= len(pairs):
                    flip(k - 1)
            for g in range(NGRP):
                read_back[g].sent(sp.after(put_back.last()).dma_start(
                    gathered[:, GB * g:GB * g + GB, :],
                    result[turn][BANK * g:BANK * g + BANK, :].rearrange("(j p) c -> p j c", p=P)))
            gate_ring = flip_ring
            def land(g):
                cols = slice(GB * g, GB * g + GB)
                return dve.did(dve.after(read_back[g].last(), shared_added[g]).tensor_tensor(
                    x[:, cols, :], x[:, cols, :], gathered[:, cols, :], ALU.add))

            for g in range(EARLY, NGRP):
                shared_up_gate(g)
            landed = [land(g) for g in range(EARLY)]
            for g in range(EARLY, NGRP):
                shared_down(g)
                landed.append(land(g))
            for e in (pe, act, dve):
                e.after(act.last(), dve.last(), put_back.last())
            return landed

        def selective_scan(landed):
            piece = carve()
            u, z, dt, dtu = (piece(NCH * NTOK).rearrange("p (c t) -> p c t", c=NCH) for _ in range(4))
            nr = 2 * DS + DR
            low = piece(NTOK, slice(2 * DS, nr))
            rest = [piece(BANK, slice(0, 2 * DS)) for _ in range(2)]
            mid16 = [piece(BANK // 2, slice(0, 2 * DS)).bitcast(BF16) for _ in range(2)]
            rows16 = piece(NTOK // 2, slice(0, 6 * DS)).bitcast(BF16)
            a_neg = piece(NCH * DS)
            piece = carve(SCAN_FIRST)
            decay = [[piece(BANK) for _ in range(2)] for _ in range(NCH)]
            state = [[piece(BANK) for _ in range(3)] for _ in range(NCH)]
            c_row = [piece(BANK) for _ in range(3)]

            conv_w, in_b = wt("conv_w"), wt("in_b")
            ring = Ring([psum[:, i, :] for i in range(8)])
            table_set(LOG_EXP)
            a_exp = act.did(nc.scalar.activation(a_neg, wt("a_log_b"), ACT.Exp))
            dve.did(dve.after(a_exp).tensor_scalar(a_neg, a_neg, -1.0, None, ALU.mult))
            conv_done, u_ready, low_ready = ([None] * NGRP for _ in range(3))
            raw_u, mid_copied = {}, [None] * 2

            def tap(c, k):
                return conv_w[:, DC * c + k:DC * c + k + 1]

            def project_u(g):
                cols = slice(BANK * g, BANK * g + BANK)
                for c in range(NCH):
                    bank, free = ring.take()
                    r = pe.did(pe.after(free, normed[g]).matmul(bank, in_b[:, P * c:P * c + P], xnt_group(g), start=True, stop=True))
                    m = act.did(act.after(r).activation(u[:, c, cols], bank, ACT.Identity, bias=wt("conv_b")[:, c:c + 1], scale=tap(c, DC - 1)))
                    raw_u[g, c] = (bank, m)

            def convolve(g):
                cols = slice(BANK * g, BANK * g + BANK)
                for c in range(NCH):
                    bank, m = raw_u[g, c]
                    raw = bank.rearrange("p (s t) -> p s t", s=2)
                    total = u[:, c, cols].rearrange("p (s t) -> p s t", s=2)
                    for back in range(1, DC):
                        m = dve.did(dve.after(m).scalar_tensor_tensor(
                            total[:, :, back:SEQ], raw[:, :, 0:SEQ - back], tap(c, DC - 1 - back), total[:, :, back:SEQ], ALU.mult, ALU.add))
                    ring.release(bank, m)
                    conv_done[g] = m

            def project_z(g):
                cols = slice(BANK * g, BANK * g + BANK)
                for c in range(NCH):
                    bank, free = ring.take()
                    r = pe.did(pe.after(free).matmul(bank, in_b[:, DI + P * c:DI + P * c + P], xnt_group(g), start=True, stop=True))
                    ring.release(bank, act.did(act.after(r).activation(z[:, c, cols], bank, ACT.Silu)))

            def silu_u(g):
                cols = slice(BANK * g, BANK * g + BANK)
                u_ready[g] = act.did(act.after(conv_done[g]).activation(u[:, :, cols], u[:, :, cols], ACT.Silu))

            def rows_of(g):
                cols = slice(BANK * g, BANK * g + BANK)
                bank, free = ring.take()
                pe.after(free, u_ready[g])
                for c in range(NCH):
                    r = nc.tensor.matmul(bank[0:nr, :], wt("x_b")[:, nr * c:nr * c + nr], u[:, c, cols], start=(c == 0), stop=(c == NCH - 1))
                r = pe.did(r)
                bc = bank[0:2 * DS, :]
                hi, mid, re = rows16[0:2 * DS, cols], mid16[g % 2], rest[g % 2]
                m_hi = act.did(act.after(r).activation(hi, bc, ACT.Copy))
                low_ready[g] = act.did(nc.scalar.activation(low[:, cols], bank[2 * DS:nr, :], ACT.Copy))
                m_re = dve.did(dve.after(m_hi, mid_copied[g % 2]).tensor_tensor(re, bc, hi, ALU.subtract))
                ring.release(bank, [m_re, low_ready[g]])
                m = dve.did(dve.after(m_re).tensor_copy(mid, re))
                mid_copied[g % 2] = act.did(act.after(m_re).activation(rows16[2 * DS:4 * DS, cols], re, ACT.Copy))
                dve.did(dve.after(m).tensor_tensor(rows16[4 * DS:6 * DS, cols], re, mid, ALU.subtract))

            norm_steps = [normalise(g, ring, False) for g in range(NGRP)]
            for g in range(NGRP):
                measure(g, landed[g])
            for root, _, _ in norm_steps:
                root()
            table_set(SILU)
            for _, scale, turn in norm_steps:
                scale()
                turn()
            project_u(0)
            for g in range(NGRP + 1):
                if g < NGRP:
                    convolve(g)
                if g + 1 < NGRP:
                    project_u(g + 1)
                if g >= 1:
                    rows_of(g - 1)
                if g < NGRP:
                    silu_u(g)
                    project_z(g)

            table_set(LOG_EXP)
            for g in range(NGRP):
                cols = slice(BANK * g, BANK * g + BANK)
                for c in range(NCH):
                    bank, free = ring.take()
                    r = pe.did(pe.after(free, low_ready[g]).matmul(
                        bank, wt("dt_w", slice(2 * DS, nr))[:, P * c:P * c + P], low[:, cols], start=True, stop=True))
                    act.after(r)
                    m = act.did(nc.scalar.activation(dt[:, c, cols], bank, ACT.Abs, bias=wt("dt_b")[:, c:c + 1]))
                    m_relu = dve.did(dve.after(r, m).tensor_scalar(dtu[:, c, cols], bank, wt("dt_b")[:, c:c + 1], 0.0, ALU.add, ALU.max))
                    ring.release(bank, m_relu)
                m = act.did(act.after(m).activation(dt[:, :, cols], dt[:, :, cols], ACT.Exp, scale=-1.0))
                m = act.did(act.after(m).activation(dt[:, :, cols], dt[:, :, cols], ACT.Ln, bias=one))
                m = dve.did(dve.after(m, m_relu).tensor_tensor(dt[:, :, cols], dt[:, :, cols], dtu[:, :, cols], ALU.add))
                pool.did(pool.after(m, u_ready[g]).tensor_tensor(dtu[:, :, cols], dt[:, :, cols], u[:, :, cols], ALU.mult))

            for c in range(NCH):
                for i in range(2):
                    starts = decay[c][i].rearrange("p (s t) -> p s t", t=SEQ)[:, :, 0:1]
                    dve.did(nc.vector.memset(starts, 0.0))
            next_layer()
            driven_bank = [[psum[:, 2 * c + i, :] for i in range(2)] for c in range(NCH)]
            c_ring = Ring([psum[:, i, :] for i in (4, 5)])
            y_bank = [psum[:, 6 + c, :] for c in range(NCH)]
            pick_row = ct("pick_row", slice(0, 6 * DS))
            steps = [(g, n) for g in range(NGRP) for n in range(DS)]
            driven_free = [[None] * 2 for _ in range(NCH)]
            decay_free = [[None] * 2 for _ in range(NCH)]
            state_free = [[None] * 3 for _ in range(NCH)]
            c_row_free = [None] * 3
            y_free = [None] * NCH
            b_ready, decay_ready, c_ready, state_ready, y_done = {}, {}, {}, {}, {}

            def prepare(s):
                g, n = steps[s]
                cols, i = slice(BANK * g, BANK * g + BANK), s % 2
                for c in range(NCH):
                    pe.after(driven_free[c][i])
                    b_ready[s, c] = pe.did(nc.tensor.matmul(driven_bank[c][i], pick_row[:, P * n:P * n + P], rows16[:, cols],
                                                            start=True, stop=True))
                bank, free = c_ring.take()
                r = pe.did(pe.after(free).matmul(bank, pick_row[:, P * (DS + n):P * (DS + n) + P], rows16[:, cols], start=True, stop=True))
                for c in range(NCH):
                    live = decay[c][i].rearrange("p (s t) -> p s t", t=SEQ)[:, :, 1:SEQ]
                    seq = dt[:, c, cols].rearrange("p (s t) -> p s t", t=SEQ)[:, :, 1:SEQ]
                    act.after(decay_free[c][i])
                    decay_ready[s, c] = act.did(nc.scalar.activation(live, seq, ACT.Exp, scale=a_neg[:, DS * c + n:DS * c + n + 1]))
                act.after(r, c_row_free[s % 3])
                c_ready[s] = act.did(nc.scalar.activation(c_row[s % 3], bank, ACT.Copy))
                c_ring.release(bank, c_ready[s])

            def recur(s):
                g, n = steps[s]
                cols, i = slice(BANK * g, BANK * g + BANK), s % 2
                driven = []
                for c in range(NCH):
                    bank = driven_bank[c][i]
                    driven.append(dve.did(dve.after(b_ready[s, c]).tensor_tensor(bank, bank, dtu[:, c, cols], ALU.mult)))
                for c in range(NCH):
                    dve.after(driven[c], decay_ready[s, c], state_free[c][s % 3])
                    m = dve.did(nc.vector.tensor_tensor_scan(state[c][s % 3], decay[c][i], driven_bank[c][i], 0.0, ALU.mult, ALU.add))
                    state_ready[s, c] = driven_free[c][i] = decay_free[c][i] = m

            def read_out(s):
                for c in range(NCH):
                    pool.after(state_ready[s, c], c_ready[s])
                    y_done[s, c] = pool.did(nc.gpsimd.tensor_tensor(state[c][s % 3], state[c][s % 3], c_row[s % 3], ALU.mult))
                c_row_free[s % 3] = y_done[s, NCH - 1]

            def add_up(s):
                g, n = steps[s]
                for c in range(NCH):
                    pe.after(y_done[s, c], y_free[c])
                    state_free[c][s % 3] = pe.did(nc.tensor.matmul(y_bank[c], ident, state[c][s % 3], start=(n == 0), stop=(n == DS - 1)))
                if n == 0:
                    y_free[:] = [None] * NCH

            def finish(g):
                cols = slice(BANK * g, BANK * g + BANK)
                summed = [state_free[c][(DS * (g + 1) - 1) % 3] for c in range(NCH)]
                mark = {}

                def skip():
                    for c in range(NCH):
                        y_free[c] = mark["y", c] = dve.did(dve.after(summed[c]).scalar_tensor_tensor(
                            u[:, c, cols], u[:, c, cols], wt("d_b")[:, c:c + 1], y_bank[c], ALU.mult, ALU.add))

                def gated(c):
                    engine = dve if g == NGRP - 1 else pool
                    mark["gated", c] = engine.did(engine.after(mark["y", c]).tensor_tensor(
                        z[:, c, cols], z[:, c, cols], u[:, c, cols], ALU.mult))

                def project_out():
                    mark["bank"], free = c_ring.take()
                    pe.after(free, mark["gated", 0], mark["gated", 1])
                    for q in range(GB):
                        j = GB * g + q
                        for c in range(NCH):
                            r = nc.tensor.matmul(mark["bank"][:, P * q:P * q + P], z[:, c, P * j:P * j + P],
                                                 wt("out_b")[:, DM * c:DM * c + DM], start=(c == 0), stop=(c == NCH - 1))
                    mark["out"] = pe.did(r)

                def add():
                    added = dve.did(dve.after(mark["out"]).tensor_tensor(x_cols[:, cols], x_cols[:, cols], mark["bank"], ALU.add))
                    c_ring.release(mark["bank"], added)
                    measure(g, added)
                return [skip, lambda: gated(0), lambda: gated(1), None, project_out, add] + normalise(g, c_ring, True)

            later = []
            for s in range(-1, len(steps) + 1):
                if s + 1 < len(steps):
                    prepare(s + 1)
                if 0 <= s < len(steps):
                    recur(s)
                    read_out(s)
                while later and later[0][0] <= s:
                    later.pop(0)[1]()
                if s >= 1:
                    add_up(s - 1)
                    if (s - 1) % DS == DS - 1:
                        later += [(s + 1 + i, work) for i, work in enumerate(finish(steps[s - 1][0])) if work]
            later.pop(0)[1]()
            rings = [Ring(banks) for banks in (driven_bank[0], driven_bank[1], y_bank)]
            for ring, marks in zip(rings, (driven_free[0], driven_free[1], y_free)):
                ring.freed = list(marks)
            return [work for _, work in later], 2, rings + [c_ring]

        landed = experts(0, *state_space())
        landed = experts(1, *selective_scan(landed))
        written = Transfers(sem("written"))
        for g in range(NGRP):
            cols = slice(BANK * g, BANK * g + BANK)
            written.sent(sp.after(landed[g]).dma_start(out[:, cols], x_cols[:, cols]))
        sp.after(written.last())


def constants():
    k, m = np.arange(P)[:, None], np.arange(P)[None, :]
    f = {
        "ident": k == m,
        "tri": np.concatenate([k <= m, np.ones((P, P))], 1),
        "shift": k == m + 1,
        "shift_in": (k == 0) & (m == P - 1),
        "rev_expert": (NE - np.arange(NE))[None, :],
        "keep": np.tile(np.arange(NBLK) != 0, NE)[None, :],
        "slot": np.arange(NSLOT)[None, :],
        "token": k + P * np.arange(NBLK)[None, :],
        "unfilled": NTOK + k + P * np.arange(NSLOT)[None, :],
    }
    row = np.arange(P)[:, None]
    mask = np.where(m < k, MASKED, 0.0)
    h = {
        "ident16": k == m,
        "tri16": k <= m,
        "ones16": np.ones((P, P)),
        "mask16": np.concatenate([mask, mask], 1),
        "pick_head": (row >= DECAY_AT) & (row < DECAY_END) & ((row - DECAY_AT) % NH == np.repeat(np.arange(NH), P)[None, :]),
        "pick_row": (row < 6 * DS) & (row % (2 * DS) == np.repeat(np.arange(2 * DS), P)[None, :]),
    }
    freq = (np.repeat([-1.0, 1.0], HALF) / 10000.0 ** (np.tile(np.arange(HALF), 2) / HALF) / (2 * np.pi)).astype(np.float32)
    freq_parts = []
    for _ in range(PARTS):
        freq_parts.append((freq.view(np.uint32) & 0xFFFF0000).view(np.float32))
        freq = freq - freq_parts[-1]
    freq16 = np.zeros((P, NH, NS), np.float32)
    for i in range(FREQ_ROWS):
        freq16[i, i % NH] = freq_parts[i // NH % PARTS]
    h["freq16"] = freq16.reshape(P, NH * NS)
    c16 = np.zeros((P, C_COLS), np.uint16)
    for name, value in h.items():
        at, width = C_AT[name]
        c16[:, at:at + width] = np.broadcast_to(value, (P, width)).astype(np.float32).view(np.uint32) >> 16
    return f, c16


def kernel(**inputs):
    import numpy as _np
    import concourse.bacc as _bacc
    from concourse import mybir as _mybir
    from concourse.bass_utils import run_bass_kernel_spmd as _run

    i = {name: _np.asarray(a) for name, a in inputs.items()}
    f32_consts, c16 = constants()

    def halves(a):
        return a.reshape(-1, P, a.shape[-1]).transpose(1, 0, 2).reshape(P, -1)

    wa = i["L0_attn_a_W_in"]
    z, xr, bm, cm, dtc = _np.split(wa, [256, 512, 768, 1024], axis=1)

    def turned(m, first, second):
        m = m.reshape(DM, NH, HALF, 2)
        return _np.concatenate([m[..., first], m[..., second]], 2).reshape(DM, NH * NS)
    nr = 2 * DS + DR
    wx = _np.concatenate([i["L0_attn_b_W_x"][DR:nr], i["L0_attn_b_W_x"][0:DR]], 0).T
    packed = {
        "in_a": _np.concatenate([z, turned(bm, 0, 1), turned(bm, 1, 0), turned(cm, 0, 1), turned(cm, 1, 0), xr, dtc], 1),
        "dt_bias": i["L0_attn_a_dt_bias"][None, :],
        "a_log_a": i["L0_attn_a_A_log"][None, :],
        "norm_w": i["L0_attn_a_norm_weight"].reshape(NPAIR, P).T,
        "out_a": halves(i["L0_attn_a_W_out"]),
        "router": i["L0_ffn_router_w"].T,
        "shared_gate": i["L0_ffn_shared_gate_w"].T,
        "shared_up": i["L0_ffn_shared_up_w"].T,
        "shared_down": halves(i["L0_ffn_shared_down_w"].T),
        "gate_up": i["L0_ffn_gate_up_proj"].transpose(1, 0, 2).reshape(P, -1),
        "down": i["L0_ffn_down_proj"].transpose(1, 0, 2).reshape(P, -1),
        "in_b": i["L0_attn_b_W_in"].T,
        "conv_w": halves(i["L0_attn_b_conv_w"]),
        "conv_b": i["L0_attn_b_conv_b"].reshape(NCH, P).T,
        "x_b": halves(wx),
        "dt_b": i["L0_attn_b_b_dt"].reshape(NCH, P).T,
        "a_log_b": halves(i["L0_attn_b_A_log"]),
        "d_b": i["L0_attn_b_D"].reshape(NCH, P).T,
        "out_b": halves(i["L0_attn_b_W_out"].T),
    }
    packed.update(f32_consts)
    w = _np.zeros((P, W_COLS), _np.float32)
    for name, value in packed.items():
        at, width = W_AT[name]
        w[:, at:at + width] = value
    at, width = W_AT["dt_w"]
    w[2 * DS:nr, at:at + width] = i["L0_attn_b_W_dt"].T
    x = i["L0_attn_a_hidden"].reshape(NBLK, P, DM).transpose(1, 0, 2).reshape(P, NBLK * DM)
    arrays = {"x_in": _np.ascontiguousarray(x), "w_in": w, "c_in": c16}

    nc = _bacc.Bacc("TRN2", target_bir_lowering=False, num_devices=1)
    args = [nc.dram_tensor(n, a.shape, _mybir.dt.from_np(a.dtype), kind="ExternalInput").ap() for n, a in arrays.items()]
    args.append(nc.dram_tensor("out_0", (P, NBLK * DM), _mybir.dt.float32, kind="ExternalOutput").ap())
    build(nc, *args)
    got = _run(nc, [arrays], core_ids=[0]).results[0]["out_0"]
    return got.reshape(P, NBLK, DM).transpose(1, 0, 2).reshape(BATCH, SEQ, DM)
```
